# Optimizing a Trainium2 kernel written in Bass

```python
import numpy as np
import jax
import jax.numpy as jnp

def _softmax(x, axis=-1):
    return jax.nn.softmax(x, axis=axis)

def _gelu(x):
    return jax.nn.gelu(x, approximate=True)

def _silu(x):
    return jax.nn.silu(x)

def _sigmoid(x):
    return jax.nn.sigmoid(x)

def _layernorm(x, axis=-1, eps=1e-05):
    m = jnp.mean(x, axis=axis, keepdims=True)
    v = jnp.var(x, axis=axis, keepdims=True)
    return (x - m) / jnp.sqrt(v + eps)

def _scatter_add(tgt, idx, src, axis=0):
    return tgt.at[idx].add(src)

def _segment_sum(src, seg, n):
    return jax.ops.segment_sum(src, seg, n)
kernel_name = 'mk_gnn_resnorm_d4_gnn_r16_63c99c'

def setup_inputs(seed: int=0):
    np.random.seed(seed)
    _w = jnp.asarray

    def _rec_inputs():
        import jax
        import jax.numpy as jnp
        _gk = jax.random.key(seed)
        x = -0.000202 + 1 * jax.random.normal(jax.random.fold_in(_gk, 1), (6250, 64), jnp.float32)
        src = jax.random.randint(jax.random.fold_in(_gk, 2), (200000,), 0, 6250, jnp.int32)
        dst = jax.random.randint(jax.random.fold_in(_gk, 3), (200000,), 0, 6250, jnp.int32)
        _o = jnp.argsort(dst, stable=True)
        src = src[_o]
        dst = dst[_o]
        edge_weight = jax.random.uniform(jax.random.fold_in(_gk, 13), (200000,), jnp.float32, 0.0, 1)
        edge_weight1 = -0.000414295 + 0.999828 * jax.random.normal(jax.random.fold_in(_gk, 14), (200000, 1), jnp.float32)
        return (x, src, dst, edge_weight, edge_weight1)
    x, src, dst, edge_weight, edge_weight1 = _rec_inputs()

    def _L0_gnn_setup():
        import jax, jax.numpy as jnp
        import numpy as np
        N_NODES = 6250
        N_EDGES = 100000
        IN_FEAT = 64
        OUT_FEAT = 64
        key = jax.random.key(seed)
        k1, k2, k3, k4, k5 = jax.random.split(key, 5)
        h = jax.random.normal(k1, (N_NODES, IN_FEAT), dtype=jnp.float32)
        src = jax.random.randint(k2, (N_EDGES,), 0, N_NODES, dtype=jnp.int32)
        dst = jax.random.randint(k3, (N_EDGES,), 0, N_NODES, dtype=jnp.int32)
        W = jax.random.normal(k4, (OUT_FEAT, 2 * IN_FEAT), dtype=jnp.float32) * (1.0 / np.sqrt(2 * IN_FEAT))
        b = jax.random.normal(k5, (OUT_FEAT,), dtype=jnp.float32) * 0.01
        return {'h': h, 'src': src, 'dst': dst, 'W': W, 'b': b}
    _L0_gnn_all = _L0_gnn_setup()
    _L0_gnn_in = {k: v for k, v in _L0_gnn_all.items() if k in ('W', 'b')}
    del _L0_gnn_all

    def _L1_gnn_setup():
        import jax, jax.numpy as jnp
        import numpy as np
        N_NODES = 6250
        N_EDGES = 100000
        DIM = 64
        LAYERS = 2
        key = jax.random.key(seed)
        k1, k2, k3, k4 = jax.random.split(key, 4)
        h = jax.random.normal(k1, (N_NODES, DIM), dtype=jnp.float32)
        w = jax.random.uniform(k2, (N_EDGES,), dtype=jnp.float32)
        src = jax.random.randint(k3, (N_EDGES,), 0, N_NODES, dtype=jnp.int32)
        dst = jax.random.randint(k4, (N_EDGES,), 0, N_NODES, dtype=jnp.int32)
        return {'h': h, 'w': w, 'src': src, 'dst': dst}
    _L1_gnn_all = _L1_gnn_setup()
    _L1_gnn_in = {k: v for k, v in _L1_gnn_all.items() if k in ()}
    del _L1_gnn_all

    def _L2_gnn_setup():
        import jax, jax.numpy as jnp
        import numpy as np
        N_NODES = 6250
        N_EDGES = 100000
        IN_FEATS = 64
        OUT_FEATS = 64
        EDGE_FEATS = 1
        key = jax.random.key(seed)
        ks = jax.random.split(key, 6)
        h = jax.random.normal(ks[0], (N_NODES, IN_FEATS), dtype=jnp.float32)
        e = jax.random.normal(ks[1], (N_EDGES, EDGE_FEATS), dtype=jnp.float32)
        src = jax.random.randint(ks[2], (N_EDGES,), 0, N_NODES, dtype=jnp.int32)
        dst = jax.random.randint(ks[3], (N_EDGES,), 0, N_NODES, dtype=jnp.int32)
        cat_dim = 2 * IN_FEATS + EDGE_FEATS
        W1 = jax.random.normal(ks[4], (cat_dim, OUT_FEATS), dtype=jnp.float32) / np.sqrt(cat_dim)
        b1 = jnp.zeros((OUT_FEATS,), dtype=jnp.float32)
        W2 = jax.random.normal(ks[5], (OUT_FEATS, OUT_FEATS), dtype=jnp.float32) / np.sqrt(OUT_FEATS)
        b2 = jnp.zeros((OUT_FEATS,), dtype=jnp.float32)
        return {'h': h, 'e': e, 'src': src, 'dst': dst, 'W1': W1, 'b1': b1, 'W2': W2, 'b2': b2}
    _L2_gnn_all = _L2_gnn_setup()
    _L2_gnn_in = {k: v for k, v in _L2_gnn_all.items() if k in ('W1', 'b1', 'W2', 'b2')}
    del _L2_gnn_all

    def _L3_gnn_setup():
        import jax, jax.numpy as jnp
        import numpy as np
        N_NODES = 6250
        N_EDGES = 100000
        D_IN, D_HID, D_OUT = (64, 128, 64)

        def _sage_conv(x, src, dst, W_l, b, W_r, num_nodes):
            msg_sum = jax.ops.segment_sum(x[src], dst, num_segments=num_nodes)
            deg = jax.ops.segment_sum(jnp.ones((src.shape[0],), dtype=x.dtype), dst, num_segments=num_nodes)
            mean = msg_sum / jnp.maximum(deg, 1.0)[:, None]
            return mean @ W_l + b + x @ W_r
        key = jax.random.key(seed)
        ks = jax.random.split(key, 6)
        x = jax.random.normal(ks[0], (N_NODES, D_IN), dtype=jnp.float32)
        edge_index = jax.random.randint(ks[1], (2, N_EDGES), 0, N_NODES, dtype=jnp.int64)
        s_in = 1.0 / np.sqrt(D_IN)
        s_hid = 1.0 / np.sqrt(D_HID)
        return {'x': x, 'edge_index': edge_index, 'W1_l': jax.random.normal(ks[2], (D_IN, D_HID), dtype=jnp.float32) * s_in, 'b1': jnp.zeros((D_HID,), dtype=jnp.float32), 'W1_r': jax.random.normal(ks[3], (D_IN, D_HID), dtype=jnp.float32) * s_in, 'W2_l': jax.random.normal(ks[4], (D_HID, D_OUT), dtype=jnp.float32) * s_hid, 'b2': jnp.zeros((D_OUT,), dtype=jnp.float32), 'W2_r': jax.random.normal(ks[5], (D_HID, D_OUT), dtype=jnp.float32) * s_hid}
    _L3_gnn_all = _L3_gnn_setup()
    _L3_gnn_in = {k: v for k, v in _L3_gnn_all.items() if k in ('W1_l', 'b1', 'W1_r', 'W2_l', 'b2', 'W2_r')}
    del _L3_gnn_all
    return {'x': x, 'src': src, 'dst': dst, 'edge_weight': edge_weight, 'edge_weight1': edge_weight1, 'L0_gnn_W': _L0_gnn_in['W'], 'L0_gnn_b': _L0_gnn_in['b'], 'L2_gnn_W1': _L2_gnn_in['W1'], 'L2_gnn_b1': _L2_gnn_in['b1'], 'L2_gnn_W2': _L2_gnn_in['W2'], 'L2_gnn_b2': _L2_gnn_in['b2'], 'L3_gnn_W1_l': _L3_gnn_in['W1_l'], 'L3_gnn_b1': _L3_gnn_in['b1'], 'L3_gnn_W1_r': _L3_gnn_in['W1_r'], 'L3_gnn_W2_l': _L3_gnn_in['W2_l'], 'L3_gnn_b2': _L3_gnn_in['b2'], 'L3_gnn_W2_r': _L3_gnn_in['W2_r']}

def reference(x, src, dst, edge_weight, edge_weight1, L0_gnn_W, L0_gnn_b, L2_gnn_W1, L2_gnn_b1, L2_gnn_W2, L2_gnn_b2, L3_gnn_W1_l, L3_gnn_b1, L3_gnn_W1_r, L3_gnn_W2_l, L3_gnn_b2, L3_gnn_W2_r):
    import jax
    import jax.numpy as jnp

    def _L0_gnn_ref(h, src, dst, W, b):
        import jax, jax.numpy as jnp
        import numpy as np
        N_NODES = 6250
        N_EDGES = 100000
        IN_FEAT = 64
        OUT_FEAT = 64
        N = h.shape[0]
        msgs = h[src]
        sums = jax.ops.segment_sum(msgs, dst, num_segments=N)
        deg = jax.ops.segment_sum(jnp.ones((src.shape[0],), h.dtype), dst, num_segments=N)
        h_N = sums / jnp.maximum(deg, 1.0)[:, None]
        h_total = jnp.concatenate([h, h_N], axis=1)
        return h_total @ W.T + b

    def _L1_gnn_ref(h, w, src, dst):
        import jax, jax.numpy as jnp
        import numpy as np
        N_NODES = 6250
        N_EDGES = 100000
        DIM = 64
        LAYERS = 2
        N = h.shape[0]
        deg = jnp.maximum(jax.ops.segment_sum(w, dst, num_segments=N), 1.0)
        norm = deg[:, None] ** (-0.5)
        embs = [h]
        for _ in range(LAYERS):
            h_norm = h * norm
            m = h_norm[src] * w[:, None]
            neigh_sum = jax.ops.segment_sum(m, dst, num_segments=N)
            h = neigh_sum * norm
            embs.append(h)
        return jnp.mean(jnp.stack(embs, axis=1), axis=1)

    def _L2_gnn_ref(h, e, src, dst, W1, b1, W2, b2):
        import jax, jax.numpy as jnp
        import numpy as np
        N_NODES = 6250
        N_EDGES = 100000
        IN_FEATS = 64
        OUT_FEATS = 64
        EDGE_FEATS = 1
        x = jnp.concatenate([h[src], h[dst], e], axis=1)
        m = jax.nn.relu(x @ W1 + b1) @ W2 + b2
        h_new = jax.ops.segment_sum(m, dst, num_segments=h.shape[0])
        return h_new

    def _L3_gnn_ref(x, edge_index, W1_l, b1, W1_r, W2_l, b2, W2_r):
        import jax, jax.numpy as jnp
        import numpy as np
        N_NODES = 6250
        N_EDGES = 100000
        D_IN, D_HID, D_OUT = (64, 128, 64)

        def _sage_conv(x, src, dst, W_l, b, W_r, num_nodes):
            msg_sum = jax.ops.segment_sum(x[src], dst, num_segments=num_nodes)
            deg = jax.ops.segment_sum(jnp.ones((src.shape[0],), dtype=x.dtype), dst, num_segments=num_nodes)
            mean = msg_sum / jnp.maximum(deg, 1.0)[:, None]
            return mean @ W_l + b + x @ W_r
        src, dst = (edge_index[0], edge_index[1])
        n = x.shape[0]
        h = jax.nn.relu(_sage_conv(x, src, dst, W1_l, b1, W1_r, n))
        out = _sage_conv(h, src, dst, W2_l, b2, W2_r, n)
        return out
    edge_index = jnp.stack([src, dst])
    x = _layernorm(x + _L0_gnn_ref(x, src, dst, L0_gnn_W, L0_gnn_b), axis=-1)
    x = _layernorm(x + _L1_gnn_ref(x, edge_weight, src, dst), axis=-1)
    x = _layernorm(x + _L2_gnn_ref(x, edge_weight1, src, dst, L2_gnn_W1, L2_gnn_b1, L2_gnn_W2, L2_gnn_b2), axis=-1)
    x = _layernorm(x + _L3_gnn_ref(x, edge_index, L3_gnn_W1_l, L3_gnn_b1, L3_gnn_W1_r, L3_gnn_W2_l, L3_gnn_b2, L3_gnn_W2_r), axis=-1)
    return x

_drawn_inputs = setup_inputs


def setup_inputs(seed=0):
    import zlib

    import numpy as np

    out = dict(_drawn_inputs(seed))
    spreads = {'L2_gnn_b1': (0.0, 0.1),
     'L2_gnn_b2': (0.0, 0.1),
     'L3_gnn_b1': (0.0, 0.1),
     'L3_gnn_b2': (0.0, 0.1)}
    factors = {'edge_weight': 4.391, 'edge_weight1': 4.537, 'L0_gnn_b': 6.643}
    for name, (base, spread) in spreads.items():
        noise = np.random.default_rng([zlib.crc32(name.encode()), seed]).standard_normal(out[name].shape)
        drawn = base * np.exp(spread * noise) if base else spread * noise
        out[name] = jnp.asarray(drawn.astype(out[name].dtype))
    for name, factor in factors.items():
        out[name] = (out[name] * factor).astype(out[name].dtype)
    return out
```

```python
from contextlib import ExitStack

import concourse.bass as bass
from concourse import mybir

F32 = mybir.dt.float32
I32 = mybir.dt.int32
ALU = mybir.AluOpType
ACT = mybir.ActivationFunctionType
AX = mybir.AxisListType

P = 128
D = 64
HID = 128
STEPS = 34
EPS = 1e-5
PASSES = 6
L0, L1A, L1B, L2, L3A, L3B = range(PASSES)


def build_program(nc, x, src, dst, edge_w, edge_e, L0_W, L0_b, L2_W1, L2_b1, L2_W2, L2_b2,
                  L3_W1_l, L3_b1, L3_W1_r, L3_W2_l, L3_b2, L3_W2_r, out):
    N_NODES = x.shape[0]
    N_EDGES = src.shape[0]
    EPP = -(-N_EDGES // (P * 2 * STEPS)) * 2 * STEPS
    EDGES = P * EPP
    TAIL = N_EDGES - (P - 1) * EPP
    CHUNKS = EPP // STEPS
    PAIRS = CHUNKS // 2
    NPP = -(-N_NODES // P)
    NODES = P * NPP
    NTAIL = N_NODES - (P - 1) * NPP
    GROUPS = 7
    GT = NPP // GROUPS
    BPP = 4
    BLK = EPP // BPP
    BLOCKS = P * BPP
    NO_NODE = 8191.0
    W65 = D + 1
    RING = 11
    ZROWS = 2 * STEPS
    assert 0 < TAIL <= EPP and GT * GROUPS == NPP and BPP * BLK == EPP and 0 < NTAIL <= NPP
    assert PAIRS * ZROWS == EPP and RING * BLK <= 2 * STEPS * D and GT * W65 <= 512 and NODES < NO_NODE

    def width(k):
        return W65 if k == L0 else D

    def dram(name, shape, dt=F32):
        return nc.dram_tensor(name, shape, dt, kind="Internal").ap()

    running65 = dram("running65", (EDGES, W65))
    running64 = dram("running64", (EDGES, D))
    running = [running65] + [running64] * (PASSES - 1)
    first_rows = dram("first_rows", (EDGES + NODES, D))
    dst_blocks = dram("dst_blocks", (BLOCKS, BLK))
    edges_upto = dram("edges_upto", (NODES + 1,))
    tables = [x] + [dram(f"table{k}", (NODES, D)) for k in range(1, PASSES)]
    dst_table = dram("dst_table", (NODES, D))

    def tiles_of(table, g):
        return table.rearrange("(p j) d -> p j d", p=P)[:, g * GT:(g + 1) * GT, :]

    with ExitStack() as ctx:
        def sb(name, shape, dt=F32):
            return ctx.enter_context(nc.sbuf_tensor(name, shape, dt))

        def pb(name, shape):
            return ctx.enter_context(nc.psum_tensor(name, shape, F32))

        def sem(name):
            return ctx.enter_context(nc.semaphore(name))

        src_all = sb("src_all", [P, EPP], I32)
        dst_int = sb("dst_int", [P, EPP], I32)
        dst_all = sb("dst_all", [P, EPP])
        same_all = sb("same_all", [P, EPP])
        w_all = sb("w_all", [P, EPP])
        e_all = dst_int[:, :].bitcast(F32)
        idx_c = [sb(f"idx_c{s}", [P, STEPS], I32) for s in range(2)]
        same_c = [sb(f"same_c{s}", [P, STEPS]) for s in range(2)]
        w_c = [sb(f"w_c{s}", [P, STEPS]) for s in range(2)]
        msg = [sb(f"msg{s}", [P, STEPS * W65]) for s in range(2)]
        frow = sb("frow", [P, 2 * STEPS * D])
        state = sb("state", [P, W65])
        dstate = sb("dstate", [P, D])
        xcur = sb("xcur", [P, NPP, D])
        ends = sb("ends", [P, NPP, W65])
        tab = sb("tab", [P, NPP, D])
        keep = sb("keep", [P, NPP, D])
        drow = sb("drow", [P, NPP, D])
        spill = sb("spill", [P, NPP, P])
        node_i = sb("node_i", [P, NPP], I32)
        node_f = sb("node_f", [P, NPP])
        blk_f = sb("blk_f", [P, NPP])
        blk_i = sb("blk_i", [P, NPP], I32)
        cnt = sb("cnt", [P, NPP])
        upto = sb("upto", [P, NPP])
        below = sb("below", [P, NPP])
        deg = sb("deg", [P, NPP])
        has = sb("has", [P, NPP])
        dinv = sb("dinv", [P, NPP])
        norm = sb("norm", [P, NPP])
        norm_has = sb("norm_has", [P, NPP])
        tmpn = sb("tmpn", [P, NPP])
        end_i = sb("end_i", [P, NPP], I32)
        start_i = sb("start_i", [P, NPP], I32)
        first_i = sb("first_i", [P, 1], I32)
        next_f = sb("next_f", [P, 1])
        cont = sb("cont", [P, 1])
        zero1 = sb("zero1", [P, 1])
        eps1 = sb("eps1", [P, 1])
        b0row = sb("b0row", [P, D])
        junk = sb("junk", [P, 512])
        firsts = sb("firsts", [P, BLOCKS])
        firsts_d = sb("firsts_d", [P, BPP, P])
        ident = sb("ident", [P, P])
        ones = sb("ones", [P, P])
        cat = sb("cat", [P, GT, 2 * D])
        catT = sb("catT", [P, GT * P])
        hidT = sb("hidT", [P, GT * P])
        r = sb("r", [P, GT, D])
        sq = sb("sq", [P, GT, D])
        stat = sb("stat", [P, GT])
        var = sb("var", [P, GT])
        std = sb("std", [P, GT])
        w0 = sb("w0", [D, 2 * D])
        w0T = sb("w0T", [2 * D, D])
        wab = sb("wab", [D, 2 * D])
        w2 = sb("w2", [D, D])
        w3 = sb("w3", [2 * D, HID])
        w3lr = sb("w3lr", [HID, 2 * D])
        b3 = sb("b3", [HID, 1])
        rows = sb("rows", [P, 5, D])
        ROW_B0, ROW_B1, ROW_B2, ROW_B3, ROW_E = range(5)

        ps_spill = [pb(f"ps_spill{i}", [P, 512]) for i in range(2)]
        ps_t = pb("ps_t", [P, 1024])
        ps_h = pb("ps_h", [P, 1024])
        ps_o = pb("ps_o", [P, 1024])

        filled = sem("filled")
        consts = sem("consts")
        dst_in = sem("dst_in")
        src_in = sem("src_in")
        e_in = sem("e_in")
        x_in = sem("x_in")
        wts_in = sem("wts_in")
        dst_float = sem("dst_float")
        dblk_out = sem("dblk_out")
        next_in = sem("next_in")
        firsts_rdy = sem("firsts_rdy")
        firsts_ps = sem("firsts_ps")
        blk_rdy = sem("blk_rdy")
        blk_row = [sem(f"blk_row{i}") for i in range(RING)]
        blk_used = sem("blk_used")
        upto_rdy = sem("upto_rdy")
        upto_out = sem("upto_out")
        below_in = sem("below_in")
        idx_rdy = sem("idx_rdy")
        w0_ps = sem("w0_ps")
        w0_rdy = sem("w0_rdy")
        zero_rdy = sem("zero_rdy")
        zero_out = sem("zero_out")
        aux_rdy = [sem(f"aux_rdy{k}") for k in range(PASSES)]
        pool_go = sem("pool_go")
        gathered = [[sem(f"gathered{k}_{s}") for s in range(2)] for k in range(PASSES)]
        summed = [sem(f"summed{k}") for k in range(PASSES)]
        stored = [[sem(f"stored{k}_{s}") for s in range(2)] for k in range(PASSES)]
        frow_in = [sem(f"frow_in{s}") for s in range(2)]
        ends_in = [sem(f"ends_in{g}") for g in range(GROUPS)]
        spilled = sem("spilled")
        joined = sem("joined")
        cat_rdy = sem("cat_rdy")
        turned = sem("turned")
        turned_sb = sem("turned_sb")
        hid_ps = sem("hid_ps")
        hid_sb = sem("hid_sb")
        prod = sem("prod")
        prod_used = sem("prod_used")
        prod_tab = sem("prod_tab")
        wdeg_rdy = sem("wdeg_rdy")
        norm_root = sem("norm_root")
        var_rdy = sem("var_rdy")
        std_rdy = sem("std_rdy")
        tab_rdy = sem("tab_rdy")
        tab_out = sem("tab_out")
        drow_rdy = sem("drow_rdy")
        drow_out = sem("drow_out")
        scattered = sem("scattered")
        b0_in = sem("b0_in")
        b0_out = sem("b0_out")
        out_done = sem("out_done")

        block = ctx.enter_context(nc.Block())

        WITH_CAT = (L0, L1B, L2, L3A)
        WITH_HID = (L3A,)
        WITH_LN = (L0, L1B, L2, L3B)
        TAB_DVE = (L0, L1A, L2)
        TAB_ACT = (L1B, L3A)

        def count(users, k, g, each=1):
            return (users.index(k) * GROUPS + g + 1) * each

        def slot3(tile, w):
            return tile[:, 0:STEPS * w].rearrange("p (t d) -> p t d", d=w)

        def frow3(s):
            return frow[:, s * STEPS * D:(s + 1) * STEPS * D].rearrange("p (t d) -> p t d", d=D)

        def ps3(ps, w, n=GT):
            return ps[:, 0:n * w].rearrange("p (j d) -> p j d", d=w)

        def per_node(col, g, w=D):
            return col[:, g * GT:(g + 1) * GT].unsqueeze(2).to_broadcast([P, GT, w])

        def per_group(col, w=D):
            return col[:, 0:GT].unsqueeze(2).to_broadcast([P, GT, w])

        def row_bc(i, n=GT):
            return rows[:, i:i + 1, :].to_broadcast([P, n, D])

        def grp(tile, g, lo=0, hi=D):
            return tile[:, g * GT:(g + 1) * GT, lo:hi]

        @block.sync
        def _(sp):
            def load_edges(tile, flat, signal):
                main = flat[0:(P - 1) * EPP].rearrange("(p t) -> p t", p=P - 1)
                sp.dma_start(tile[0:P - 1, :], main).then_inc(signal, 16)
                last = flat[(P - 1) * EPP:N_EDGES].rearrange("(p t) -> p t", p=1)
                sp.dma_start(tile[P - 1:P, 0:TAIL], last).then_inc(signal, 16)

            sp.wait_ge(filled, 1)
            load_edges(dst_int, dst, dst_in)
            sp.wait_ge(filled, 3)
            load_edges(src_all, src, src_in)
            load_edges(w_all, edge_w, src_in)
            sp.wait_ge(filled, 4)
            sp.dma_start(xcur[0:P - 1, :, :], x[0:(P - 1) * NPP, :].rearrange("(p j) d -> p j d", p=P - 1))\
              .then_inc(x_in, 16)
            sp.dma_start(xcur[P - 1:P, 0:NTAIL, :],
                         x[(P - 1) * NPP:N_NODES, :].rearrange("(p j) d -> p j d", p=1)).then_inc(x_in, 16)
            sp.wait_ge(dst_float, 1)
            sp.dma_start(dst_blocks.rearrange("(p b) t -> p (b t)", p=P), dst_all[:, :]).then_inc(dblk_out, 16)
            sp.wait_ge(filled, 5)
            sp.dma_start(next_f[0:P - 1, :], dst_all[1:P, 0:1]).then_inc(next_in, 16)
            sp.wait_ge(zero_rdy, 1)
            load_edges(e_all, edge_e, e_in)
            sp.wait_ge(upto_rdy, 1)
            sp.dma_start(edges_upto[1:NODES + 1].rearrange("(p j) -> p j", p=P), upto[:, :]).then_inc(upto_out, 16)
            sp.dma_start(edges_upto[0:1].rearrange("(p j) -> p j", p=1), zero1[0:1, :]).then_inc(upto_out, 16)
            sp.wait_ge(upto_out, 32)
            sp.dma_start(below[:, :], edges_upto[0:NODES].rearrange("(p j) -> p j", p=P)).then_inc(below_in, 16)

            first3 = first_rows[0:EDGES, :].rearrange("(p t) d -> p t d", p=P)

            def store(k, s, pair):
                w = width(k)
                rows_of = running[k].rearrange("(p t) d -> p (t d)", p=P)
                sp.wait_ge(summed[k], 2 * pair + s + 1)
                sp.dma_start(rows_of[:, bass.ds((2 * pair + s) * (STEPS * w), STEPS * w)],
                             msg[s][:, 0:STEPS * w]).then_inc(stored[k][s], 16)

            def load_first(s, pair):
                flat = first_rows[0:EDGES, :].rearrange("(p t) d -> p (t d)", p=P)
                sp.dma_start(frow[:, s * STEPS * D:(s + 1) * STEPS * D],
                             flat[:, bass.ds((2 * pair + s) * (STEPS * D), STEPS * D)]).then_inc(frow_in[s], 16)

            def zero_first(pair):
                flat = first_rows[0:EDGES, :].rearrange("(p t) d -> p (t d)", p=P)
                sp.dma_start(flat[:, bass.ds(pair * (ZROWS * D), ZROWS * D)], frow[:, :]).then_inc(zero_out, 16)

            for k in range(PASSES):
                if k == L2:
                    sp.wait_ge(scattered, 16 * NPP)
                    sp.wait_ge(b0_in, 16)
                    sp.dma_start(first3[:, 0, :], b0row[:, :]).then_inc(b0_out, 16)
                    sp.wait_ge(b0_out, 16)
                    load_first(0, 0)
                    load_first(1, 0)
                if k == L1A:
                    sp.wait_ge(zero_rdy, 2)
                with sp.Fori(0, PAIRS - 1) as pair:
                    for s in range(2):
                        store(k, s, pair)
                        if k == L2:
                            load_first(s, pair + 1)
                    if k == L1A:
                        zero_first(pair)
                for s in range(2):
                    store(k, s, PAIRS - 1)
                if k == L1A:
                    zero_first(PAIRS - 1)
                for g in range(GROUPS):
                    if k in TAB_DVE:
                        sp.wait_ge(tab_rdy, count(TAB_DVE, k, g))
                        source = xcur if k == L2 else tab
                        sp.dma_start(tiles_of(tables[k + 1], g), grp(source, g)).then_inc(tab_out, 16)
                    if k in TAB_ACT:
                        sp.wait_ge(prod_tab, count(TAB_ACT, k, g))
                        sp.dma_start(tiles_of(tables[k + 1], g), grp(tab, g)).then_inc(tab_out, 16)
                    if k == L1B:
                        sp.wait_ge(drow_rdy, g + 1)
                        sp.dma_start(tiles_of(dst_table, g), grp(drow, g)).then_inc(drow_out, 16)
                    if k == L3B:
                        sp.wait_ge(tab_rdy, len(TAB_DVE) * GROUPS + g + 1)
                        lo, hi = g * GT, (g + 1) * GT
                        main = out[0:(P - 1) * NPP, :].rearrange("(p j) d -> p j d", p=P - 1)
                        sp.dma_start(main[:, lo:hi, :], xcur[0:P - 1, lo:hi, :]).then_inc(out_done, 16)
                        last = min(hi, NTAIL)
                        if last > lo:
                            tail = out[(P - 1) * NPP:N_NODES, :].rearrange("(p j) d -> p j d", p=1)
                            sp.dma_start(tail[:, lo:last, :], xcur[P - 1:P, lo:last, :]).then_inc(out_done, 16)
            sp.wait_ge(out_done, 16 * (GROUPS + -(-NTAIL // GT)))
            sp.wait_ge(zero_out, 16 * PAIRS)

        @block.gpsimd
        def _(pool):
            pool.memset(dst_int[:, :], int(NO_NODE)).then_inc(filled, 1)
            pool.memset(src_all[:, :], 0).then_inc(filled, 1)
            pool.memset(w_all[:, :], 0.0).then_inc(filled, 1)
            pool.memset(xcur[:, :, :], 0.0).then_inc(filled, 1)
            pool.memset(next_f[:, :], -1.0).then_inc(filled, 1)
            pool.memset(ident[:, :], 0.0).then_inc(consts, 1)
            pool.memset(ones[:, :], 1.0).then_inc(consts, 1)
            pool.memset(zero1[:, :], 0.0).then_inc(consts, 1)
            pool.memset(eps1[:, :], EPS).then_inc(consts, 1)
            pool.iota(node_i[:, :], pattern=[[1, NPP]], base=0, channel_multiplier=NPP).then_inc(consts, 1)
            pool.iota(spill[:, :, :].bitcast(I32), pattern=[[1, NPP], [NPP, P]], base=0,
                      channel_multiplier=0).then_inc(consts, 1)
            pool.wait_ge(consts, 6)
            pool.affine_select(out=ident[:, :], in_=ident[:, :], compare_op=ALU.not_equal, fill=1.0, base=0,
                               pattern=[[-1, P]], channel_multiplier=1).then_inc(consts, 1)

            pool.wait_ge(dblk_out, 16)
            pool.wait_ge(blk_rdy, 1)
            for j in range(NPP):
                if j >= RING:
                    pool.wait_ge(blk_used, j - RING + 1)
                pool.indirect_dma_start(frow[:, (j % RING) * BLK:(j % RING + 1) * BLK], None, dst_blocks[:, :],
                                        bass.IndirectOffsetOnAxis(blk_i[:, j:j + 1], 0))\
                    .then_inc(blk_row[j % RING], 16)

            def gather_chunk(k, s):
                for t in range(STEPS):
                    pool.indirect_dma_start(slot3(msg[s], width(k))[:, t, 0:D], None, tables[k][:, :],
                                            bass.IndirectOffsetOnAxis(idx_c[s][:, t:t + 1], 0))\
                        .then_inc(gathered[k][s], 16)

            for k in range(PASSES):
                if k > 0:
                    pool.wait_ge(tab_out, 16 * k * GROUPS)
                for s in range(2):
                    pool.wait_ge(aux_rdy[k], s + 1)
                    gather_chunk(k, s)
                with pool.Fori(0, PAIRS - 1) as pair:
                    for s in range(2):
                        pool.wait_ge(stored[k][s], (pair + 1) * 16)
                        pool.wait_ge(aux_rdy[k], pair * 2 + (s + 3))
                        pool.sem_inc(pool_go, 1)
                        gather_chunk(k, s)
                for s in range(2):
                    pool.wait_ge(stored[k][s], 16 * PAIRS)
                if k == L0:
                    pool.wait_ge(idx_rdy, 1)
                else:
                    pool.wait_ge(joined, k * GROUPS)
                for j in range(NPP):
                    pool.indirect_dma_start(ends[:, j, 0:width(k)], None, running[k][:, :],
                                            bass.IndirectOffsetOnAxis(end_i[:, j:j + 1], 0))\
                        .then_inc(ends_in[j // GT], 16)
                if k == L1B:
                    pool.wait_ge(zero_out, 16 * PAIRS)
                    for j in range(NPP):
                        if j % GT == 0:
                            pool.wait_ge(drow_rdy, j // GT + 1)
                        pool.indirect_dma_start(first_rows[:, :], bass.IndirectOffsetOnAxis(start_i[:, j:j + 1], 0),
                                                drow[:, j, :], None).then_inc(scattered, 16)
                    pool.wait_ge(drow_out, 16 * GROUPS)
                    pool.indirect_dma_start(b0row[:, :], None, dst_table[:, :],
                                            bass.IndirectOffsetOnAxis(first_i[:, 0:1], 0)).then_inc(b0_in, 16)

        @block.scalar
        def _(act):
            act.dma_start(w0[:, :], L0_W).then_inc(wts_in, 16)
            act.dma_start(wab[:, 0:D], L2_W1[0:D, :]).then_inc(wts_in, 16)
            act.dma_start(wab[:, D:2 * D], L2_W1[D:2 * D, :]).then_inc(wts_in, 16)
            act.dma_start(w2[:, :], L2_W2).then_inc(wts_in, 16)
            act.dma_start(w3[0:D, :], L3_W1_l).then_inc(wts_in, 16)
            act.dma_start(w3[D:2 * D, :], L3_W1_r).then_inc(wts_in, 16)
            act.dma_start(w3lr[:, 0:D], L3_W2_l).then_inc(wts_in, 16)
            act.dma_start(w3lr[:, D:2 * D], L3_W2_r).then_inc(wts_in, 16)
            act.dma_start(b3[:, :], L3_b1.rearrange("(p a) -> p a", a=1)).then_inc(wts_in, 16)
            for i, b in ((ROW_B0, L0_b), (ROW_B1, L2_b1), (ROW_B2, L2_b2), (ROW_B3, L3_b2)):
                act.dma_start(rows[:, i, :], b.partition_broadcast(P)).then_inc(wts_in, 16)
            act.dma_start(rows[:, ROW_E, :], L2_W1[2 * D, :].partition_broadcast(P)).then_inc(wts_in, 16)

            def aux(k, s, pair):
                at = bass.ds((2 * pair + s) * STEPS, STEPS)
                if k in (L0, L1A, L1B):
                    act.copy(w_c[s][:, :], w_all[:, at])
                if k == L2:
                    act.copy(w_c[s][:, :], e_all[:, at])
                act.copy(same_c[s][:, :], same_all[:, at])
                act.copy(idx_c[s][:, :], src_all[:, at])
                act.drain()
                act.sem_inc(aux_rdy[k], 1)

            def first_chunks(k):
                if k == L0:
                    act.wait_ge(src_in, 64)
                    act.wait_ge(dst_float, 3)
                else:
                    act.wait_ge(summed[k - 1], CHUNKS)
                if k == L2:
                    act.wait_ge(e_in, 32)
                aux(k, 0, 0)
                aux(k, 1, 0)

            def root(k, g):
                act.wait_ge(var_rdy, count(WITH_LN, k, g))
                act.activation(std[:, :], var[:, :], ACT.Sqrt, bias=eps1[:, :], scale=1.0 / D)\
                   .then_inc(std_rdy, 1)

            first_chunks(L0)
            act.wait_ge(w0_ps, 1)
            act.copy(w0T[:, :], ps_t[:, 0:D]).then_inc(w0_rdy, 1)
            for k in range(PASSES):
                if k > 0:
                    first_chunks(k)
                with act.Fori(0, PAIRS - 1) as pair:
                    for s in range(2):
                        act.wait_ge(summed[k], pair * 2 + (s + 1))
                        aux(k, s, pair + 1)
                for g in range(GROUPS):
                    if k == L1B:
                        root(k, g)
                    if k in WITH_CAT:
                        kr = D if k in (L1B, L2) else 2 * D
                        act.wait_ge(turned, count(WITH_CAT, k, g))
                        if (k, g) != (WITH_CAT[0], 0):
                            act.wait_ge(prod, count(WITH_CAT, k, g) - 1)
                        act.copy(catT[0:kr, :], ps_t[0:kr, 0:GT * P]).then_inc(turned_sb, 1)
                    if k in WITH_HID:
                        act.wait_ge(hid_ps, count(WITH_HID, k, g))
                        act.activation(hidT[:, :], ps_h[:, 0:GT * P], ACT.Relu, bias=b3[:, :])\
                           .then_inc(hid_sb, 1)
                    if k in TAB_ACT:
                        act.wait_ge(prod, count(WITH_CAT, k, g))
                        act.copy(grp(tab, g), ps3(ps_o, 2 * D)[:, :, 0:D]).then_inc(prod_tab, 1)
                    if k == L0:
                        act.wait_ge(wdeg_rdy, g + 1)
                        act.activation(norm[:, g * GT:(g + 1) * GT], tmpn[:, g * GT:(g + 1) * GT], ACT.Sqrt)\
                           .then_inc(norm_root, 1)
                    if k in (L0, L2, L3B):
                        root(k, g)

        @block.tensor
        def _(pe):
            pe.wait_ge(firsts_rdy, 1)
            pe.matmul(ps_o[:, 0:BLOCKS], ones[:, :], firsts_d[:, :, :].rearrange("p b q -> p (b q)"),
                      start=True, stop=True).then_inc(firsts_ps, 1)
            pe.wait_ge(wts_in, 14 * 16)
            pe.transpose(ps_t[:, 0:D], w0[:, :], ident[0:D, 0:D]).then_inc(w0_ps, 1)
            pe.wait_ge(w0_rdy, 1)

            def carry(k, g):
                w = width(k)
                if k == L0:
                    pe.wait_ge(idx_rdy, 1)
                pe.wait_ge(summed[k], CHUNKS)
                if (k, g) >= (L0, 2):
                    pe.wait_ge(joined, k * GROUPS + g - 1)
                for j in range(GT):
                    ins = pe.matmul(ps_spill[(k * GROUPS + g) % 2][:, j * w:(j + 1) * w], spill[:, g * GT + j, :],
                                    state[:, 0:w], start=True, stop=True)
                ins.then_inc(spilled, 1)

            for k in range(PASSES):
                carry(k, 0)
                carry(k, 1)
                for g in range(GROUPS):
                    if k in WITH_CAT:
                        kr = D if k in (L1B, L2) else 2 * D
                        pe.wait_ge(cat_rdy, count(WITH_CAT, k, g))
                        if (k, g) != (WITH_CAT[0], 0):
                            pe.wait_ge(turned_sb, count(WITH_CAT, k, g) - 1)
                        for j in range(GT):
                            rows_in = xcur[:, g * GT + j, :] if k == L1B else cat[:, j, 0:kr]
                            ins = pe.transpose(ps_t[0:kr, j * P:(j + 1) * P], rows_in, ident[:, :])
                        ins.then_inc(turned, 1)
                        pe.wait_ge(turned_sb, count(WITH_CAT, k, g))
                        if k in WITH_HID:
                            for lo in range(0, GT * P, 512):
                                hi = min(lo + 512, GT * P)
                                ins = pe.matmul(ps_h[:, lo:hi], w3[:, :], catT[:, lo:hi], start=True, stop=True)
                            ins.then_inc(hid_ps, 1)
                            pe.wait_ge(hid_sb, count(WITH_HID, k, g))
                        if (k, g) != (WITH_CAT[0], 0):
                            pe.wait_ge(prod_used, count(WITH_CAT, k, g) - 1)
                        for j in range(GT):
                            at = slice(j * P, (j + 1) * P)
                            if k == L0:
                                ins = pe.matmul(ps_o[:, j * D:(j + 1) * D], catT[:, at], w0T[:, :],
                                                start=True, stop=True)
                            elif k == L1B:
                                ins = pe.matmul(ps_o[:, at], catT[0:D, at], wab[:, :], start=True, stop=True)
                            elif k == L2:
                                ins = pe.matmul(ps_o[:, j * D:(j + 1) * D], catT[0:D, at], w2[:, :],
                                                start=True, stop=True)
                            else:
                                ins = pe.matmul(ps_o[:, at], hidT[:, at], w3lr[:, :], start=True, stop=True)
                        ins.then_inc(prod, 1)
                    if g + 2 < GROUPS:
                        carry(k, g + 2)

        @block.vector
        def _(v):
            v.wait_ge(dst_in, 32)
            v.tensor_copy(dst_all[:, :], dst_int[:, :]).then_inc(dst_float, 1)
            v.memset(same_all[:, 0:1], 0.0).then_inc(dst_float, 1)
            v.drain()
            v.sem_inc(zero_rdy, 1)
            v.tensor_tensor(same_all[:, 1:EPP], dst_all[:, 1:EPP], dst_all[:, 0:EPP - 1], ALU.is_equal)\
             .then_inc(dst_float, 1)
            v.wait_ge(consts, 7)
            for b in range(BPP):
                v.tensor_scalar(firsts_d[:, b, :], ident[:, :], dst_all[:, b * BLK:b * BLK + 1], None, ALU.mult)
            v.tensor_copy(node_f[:, :], node_i[:, :])
            v.tensor_copy(first_i[:, :], dst_all[:, 0:1])
            v.drain()
            v.sem_inc(firsts_rdy, 1)
            v.wait_ge(firsts_ps, 1)
            v.tensor_copy(firsts[:, :], ps_o[:, 0:BLOCKS])
            v.drain()
            for j in range(NPP):
                v.tensor_scalar(junk[:, 0:BLOCKS], firsts[:, :], node_f[:, j:j + 1], None, ALU.is_le, ALU.add,
                                accum_out=cnt[:, j:j + 1])
                v.drain()
            v.tensor_scalar(blk_f[:, :], cnt[:, :], -1.0, 0.0, ALU.add, ALU.max)
            v.drain()
            v.tensor_copy(blk_i[:, :], blk_f[:, :]).then_inc(blk_rdy, 1)
            for j in range(NPP):
                v.wait_ge(blk_row[j % RING], 16 * (j // RING + 1))
                v.tensor_scalar(junk[:, 0:BLK], frow[:, (j % RING) * BLK:(j % RING + 1) * BLK], node_f[:, j:j + 1],
                                None, ALU.is_le, ALU.add, accum_out=cnt[:, j:j + 1]).then_inc(blk_used, 1)
                v.drain()
            v.scalar_tensor_tensor(upto[:, :], blk_f[:, :], float(BLK), cnt[:, :], ALU.mult, ALU.add)\
             .then_inc(upto_rdy, 1)
            v.memset(frow[:, :], 0.0)
            v.wait_ge(next_in, 16)
            v.tensor_tensor(cont[:, :], next_f[:, :], dst_all[:, EPP - 1:EPP], ALU.is_equal)
            v.drain()
            v.sem_inc(zero_rdy, 1)
            v.tensor_scalar(spill[:, :, :], spill[:, :, :].bitcast(I32), dst_all[:, EPP - 1:EPP], cont[:, 0:1],
                            ALU.is_equal, ALU.mult)
            v.wait_ge(below_in, 16)
            v.tensor_tensor(deg[:, :], upto[:, :], below[:, :], ALU.subtract)
            v.tensor_scalar(tmpn[:, :], upto[:, :], -1.0, 0.0, ALU.add, ALU.max)
            v.drain()
            v.tensor_copy(end_i[:, :], tmpn[:, :])
            v.tensor_scalar(has[:, :], deg[:, :], 1.0, None, ALU.min)
            v.tensor_scalar(dinv[:, :], deg[:, :], 1.0, None, ALU.max)
            v.tensor_scalar(cnt[:, :], node_f[:, :], float(EDGES), None, ALU.add)
            v.drain()
            v.reciprocal(dinv[:, :], dinv[:, :])
            v.tensor_tensor(below[:, :], below[:, :], cnt[:, :], ALU.subtract)
            v.drain()
            v.tensor_tensor(dinv[:, :], dinv[:, :], has[:, :], ALU.mult)
            v.tensor_tensor(below[:, :], below[:, :], has[:, :], ALU.mult)
            v.drain()
            v.tensor_tensor(below[:, :], below[:, :], cnt[:, :], ALU.add)
            v.drain()
            v.tensor_copy(start_i[:, :], below[:, :])
            v.wait_ge(x_in, 32)
            v.wait_ge(wts_in, 14 * 16)
            v.tensor_tensor(keep[:, :, :], xcur[:, :, :], row_bc(ROW_B0, NPP), ALU.add)
            v.drain()
            v.sem_inc(idx_rdy, 1)

            def chunk(k, s, pair):
                w = width(k)
                m = slot3(msg[s], w)
                v.wait_ge(aux_rdy[k], pair * 2 + (s + 1))
                v.wait_ge(gathered[k][s], (pair + 1) * (16 * STEPS))
                if k == L0:
                    v.tensor_copy(m[:, :, D:D + 1], w_c[s][:, :].unsqueeze(2))
                    v.drain()
                if k in (L1A, L1B):
                    v.tensor_tensor(m, m, w_c[s][:, :].unsqueeze(2).to_broadcast([P, STEPS, D]), ALU.mult)
                    v.drain()
                if k == L2:
                    f = frow3(s)
                    v.wait_ge(frow_in[s], (pair + 1) * 16)
                    for t in range(STEPS):
                        v.scalar_tensor_tensor(f[:, t, :], dstate[:, :] if t == 0 else f[:, t - 1, :],
                                               same_c[s][:, t:t + 1], f[:, t, :], ALU.mult, ALU.add)
                        v.scalar_tensor_tensor(m[:, t, :], rows[:, ROW_E, :], w_c[s][:, t:t + 1], m[:, t, :],
                                               ALU.mult, ALU.add)
                        v.drain()
                    v.tensor_tensor(m, m, f, ALU.add)
                    v.tensor_copy(dstate[:, :], f[:, STEPS - 1, :])
                    v.drain()
                    v.tensor_scalar(m, m, 0.0, None, ALU.max)
                    v.drain()
                for t in range(STEPS):
                    v.scalar_tensor_tensor(m[:, t, :], state[:, 0:w] if t == 0 else m[:, t - 1, :],
                                           same_c[s][:, t:t + 1], m[:, t, :], ALU.mult, ALU.add)
                    v.drain()
                v.tensor_copy(state[:, 0:w], m[:, STEPS - 1, :])
                v.drain()
                v.sem_inc(summed[k], 1)

            def join(k, g):
                w = width(k)
                v.wait_ge(ends_in[g], 16 * GT * (k + 1))
                v.wait_ge(spilled, k * GROUPS + g + 1)
                v.tensor_tensor(grp(ends, g, 0, w), grp(ends, g, 0, w), ps3(ps_spill[(k * GROUPS + g) % 2], w),
                                ALU.add)
                v.drain()
                v.sem_inc(joined, 1)
                total = grp(ends, g)
                if k == L0:
                    if g > 0:
                        v.wait_ge(turned, count(WITH_CAT, k, g) - 1)
                    v.tensor_tensor(cat[:, :, D:2 * D], total, per_node(dinv, g), ALU.mult)
                    v.tensor_copy(cat[:, :, 0:D], grp(xcur, g))
                    v.tensor_tensor(tmpn[:, g * GT:(g + 1) * GT], grp(ends, g, D, D + 1).squeeze(2),
                                    has[:, g * GT:(g + 1) * GT], ALU.mult)
                    v.drain()
                    v.sem_inc(cat_rdy, 1)
                    v.tensor_scalar(tmpn[:, g * GT:(g + 1) * GT], tmpn[:, g * GT:(g + 1) * GT], 1.0, None, ALU.max)
                    v.drain()
                    v.sem_inc(wdeg_rdy, 1)
                elif k == L2:
                    v.wait_ge(turned, count(WITH_CAT, k, g) - 1)
                    v.tensor_tensor(cat[:, :, 0:D], total, per_node(has, g), ALU.mult)
                    v.drain()
                    v.sem_inc(cat_rdy, 1)
                elif k == L3A:
                    v.wait_ge(turned, count(WITH_CAT, k, g) - 1)
                    v.tensor_tensor(cat[:, :, 0:D], total, per_node(dinv, g), ALU.mult)
                    v.tensor_copy(cat[:, :, D:2 * D], grp(xcur, g))
                    v.drain()
                    v.sem_inc(cat_rdy, 1)

            def layernorm(k, g):
                v.tensor_reduce(stat[:, :], r[:, :, :], AX.X, ALU.add)
                v.drain()
                v.tensor_scalar(stat[:, :], stat[:, :], -1.0 / D, None, ALU.mult)
                v.drain()
                v.tensor_tensor(r[:, :, :], r[:, :, :], per_group(stat), ALU.add)
                v.drain()
                v.tensor_tensor(sq[:, :, :], r[:, :, :], r[:, :, :], ALU.mult)
                v.drain()
                v.tensor_reduce(var[:, :], sq[:, :, :], AX.X, ALU.add).then_inc(var_rdy, 1)
                v.wait_ge(std_rdy, count(WITH_LN, k, g))
                v.reciprocal(stat[:, :], std[:, :])
                v.drain()
                v.tensor_tensor(grp(xcur, g), r[:, :, :], per_group(stat), ALU.mult)
                v.drain()

            def finish(k, g):
                at = slice(g * GT, (g + 1) * GT)
                total = grp(ends, g)
                if k == L0:
                    v.wait_ge(prod, count(WITH_CAT, k, g))
                    v.tensor_tensor(r[:, :, :], ps3(ps_o, D), grp(keep, g), ALU.add)
                    v.drain()
                    v.sem_inc(prod_used, 1)
                    layernorm(k, g)
                    v.wait_ge(norm_root, g + 1)
                    v.reciprocal(norm[:, at], norm[:, at])
                    v.drain()
                    v.tensor_tensor(norm_has[:, at], norm[:, at], has[:, at], ALU.mult)
                    v.tensor_tensor(grp(tab, g), grp(xcur, g), per_node(norm, g), ALU.mult)
                    v.drain()
                    v.sem_inc(tab_rdy, 1)
                elif k == L1A:
                    v.tensor_tensor(total, total, per_node(norm_has, g), ALU.mult)
                    v.drain()
                    if g == 0:
                        v.wait_ge(tab_out, 16 * GROUPS)
                    v.tensor_tensor(grp(tab, g), total, per_node(norm, g), ALU.mult)
                    v.tensor_tensor(grp(keep, g), total, grp(xcur, g), ALU.add)
                    v.drain()
                    v.sem_inc(tab_rdy, 1)
                elif k == L1B:
                    v.tensor_tensor(r[:, :, :], total, per_node(norm_has, g), ALU.mult)
                    v.drain()
                    v.tensor_tensor(r[:, :, :], r[:, :, :], grp(keep, g), ALU.add)
                    v.drain()
                    v.scalar_tensor_tensor(r[:, :, :], r[:, :, :], 1.0 / 3.0, grp(xcur, g), ALU.mult, ALU.add)
                    v.drain()
                    layernorm(k, g)
                    v.sem_inc(cat_rdy, 1)
                elif k == L2:
                    v.tensor_tensor(sq[:, :, :], row_bc(ROW_B2), per_node(deg, g), ALU.mult)
                    v.drain()
                    v.tensor_tensor(sq[:, :, :], sq[:, :, :], grp(xcur, g), ALU.add)
                    v.drain()
                    v.wait_ge(prod, count(WITH_CAT, k, g))
                    v.tensor_tensor(r[:, :, :], ps3(ps_o, D), sq[:, :, :], ALU.add)
                    v.drain()
                    v.sem_inc(prod_used, 1)
                    layernorm(k, g)
                    v.sem_inc(tab_rdy, 1)
                elif k == L3A:
                    v.wait_ge(prod_tab, count(TAB_ACT, k, g))
                    v.tensor_tensor(r[:, :, :], ps3(ps_o, 2 * D)[:, :, D:2 * D], row_bc(ROW_B3), ALU.add)
                    v.drain()
                    v.sem_inc(prod_used, 1)
                    v.tensor_tensor(grp(keep, g), r[:, :, :], grp(xcur, g), ALU.add)
                    v.drain()
                elif k == L3B:
                    v.tensor_tensor(r[:, :, :], total, per_node(dinv, g), ALU.mult)
                    v.drain()
                    v.tensor_tensor(r[:, :, :], r[:, :, :], grp(keep, g), ALU.add)
                    v.drain()
                    layernorm(k, g)
                    v.sem_inc(tab_rdy, 1)

            def dst_half(g):
                v.wait_ge(prod_tab, count(TAB_ACT, L1B, g))
                v.tensor_tensor(grp(drow, g), ps3(ps_o, 2 * D)[:, :, D:2 * D], row_bc(ROW_B1), ALU.add)
                v.drain()
                v.sem_inc(prod_used, 1)
                v.sem_inc(drow_rdy, 1)

            for k in range(PASSES):
                if k > 0:
                    v.wait_ge(spilled, k * GROUPS)
                v.memset(state[:, :], 0.0)
                v.memset(dstate[:, :], 0.0)
                v.drain()
                with v.Fori(0, PAIRS) as pair:
                    for s in range(2):
                        chunk(k, s, pair)
                join(k, 0)
                for g in range(GROUPS):
                    if g + 1 < GROUPS:
                        join(k, g + 1)
                    finish(k, g)
                    if k == L1B and g > 0:
                        dst_half(g - 1)
                if k == L1B:
                    dst_half(GROUPS - 1)


_INS = ["x", "src", "dst", "edge_weight", "edge_weight1", "L0_gnn_W", "L0_gnn_b", "L2_gnn_W1", "L2_gnn_b1",
        "L2_gnn_W2", "L2_gnn_b2", "L3_gnn_W1_l", "L3_gnn_b1", "L3_gnn_W1_r", "L3_gnn_W2_l", "L3_gnn_b2",
        "L3_gnn_W2_r"]


def kernel(**inputs):
    import numpy as _np
    import concourse.bacc as _bacc
    from concourse.bass_utils import run_bass_kernel_spmd as _run

    nc = _bacc.Bacc("TRN2", target_bir_lowering=False, num_devices=1)
    arrays, args = {}, []
    for name in _INS:
        a = _np.ascontiguousarray(inputs[name])
        if name == "edge_weight1":
            a = a.reshape(-1)
        arrays[f"in_{name}"] = a
        args.append(nc.dram_tensor(f"in_{name}", a.shape, mybir.dt.from_np(a.dtype), kind="ExternalInput").ap())
    out = nc.dram_tensor("out_x", arrays["in_x"].shape, F32, kind="ExternalOutput").ap()
    build_program(nc, *args, out)
    return _run(nc, [arrays], core_ids=[0]).results[0]["out_x"]
```

```python
from contextlib import ExitStack

import concourse.bass as bass
from concourse import mybir

F32 = mybir.dt.float32
BF16 = mybir.dt.bfloat16
F16 = mybir.dt.float16
I32 = mybir.dt.int32
ALU = mybir.AluOpType
ACT = mybir.ActivationFunctionType
AX = mybir.AxisListType

P = 128
Q = 125
D = 64
HID = 128
STEPS = 34
GNODES = 5
SLOTS = 256
EPS = 1e-5
PASSES = 6
L0, L1A, L1B, L2, L3A, L3B = range(PASSES)


def build_program(nc, x, src, dst, edge_w, edge_e, L0_W, L0_b, L2_W1, L2_b1, L2_W2, L2_b2,
                  L3_W1_l, L3_b1, L3_W1_r, L3_W2_l, L3_b2, L3_W2_r, out):
    N_NODES = x.shape[0]
    N_EDGES = src.shape[0]
    EPP = -(-N_EDGES // (P * 2 * STEPS)) * 2 * STEPS
    EDGES = P * EPP
    TAIL = N_EDGES - (P - 1) * EPP
    CHUNKS = EPP // STEPS
    PAIRS = CHUNKS // 2
    NPP = N_NODES // Q
    GT = 5
    GROUPS = NPP // GT
    BPP = 4
    BLK = EPP // BPP
    BLOCKS = P * BPP
    NO_NODE = 8191.0
    RING = 11
    ZROWS = 23
    ZSTORES = EPP // ZROWS
    HALVES = SLOTS // P
    NGROUPS = N_NODES // GNODES
    GBLK = NGROUPS // Q
    COLS = NPP * GNODES
    BATCH = 5
    BT = BATCH * HALVES
    GPB = Q // GNODES
    ITG = 2 * GPB
    ITB = ITG // BATCH
    TURNS = NGROUPS // ITG
    BANK = 512
    BUILD_BANKS = 5
    FAR = 10000.0
    AROW = NPP * Q
    assert 0 < TAIL <= EPP and NPP * Q == N_NODES and GT * GROUPS == NPP and BPP * BLK == EPP
    assert ZSTORES * ZROWS == EPP and RING * BLK <= 2 * STEPS * D and GT * D <= BANK and N_NODES < NO_NODE
    assert NGROUPS * GNODES == N_NODES and GBLK * Q == NGROUPS and TURNS * ITG == NGROUPS
    assert COLS <= 256 and ITG % BUILD_BANKS == 0 and ITB % 2 == 0 and ZSTORES > 2 * TURNS

    COUNTS, WEIGHTS = "counts", "weights"
    MATRIX = {L0: COUNTS, L1A: WEIGHTS, L1B: WEIGHTS, L3A: COUNTS, L3B: COUNTS}

    def dram(name, shape, dt=F32):
        return nc.dram_tensor(name, shape, dt, kind="Internal").ap()

    running = dram("running", (EDGES, D))
    running_w = dram("running_w", (EDGES, 1))
    first_rows = dram("first_rows", (EDGES + N_NODES, D))
    dst_blocks = dram("dst_blocks", (BLOCKS, BLK))
    edges_upto = dram("edges_upto", (N_NODES + 2 * GNODES,))
    packed = [dram(f"packed{i}", (EDGES + SLOTS, 1)) for i in range(3)]
    tables = [x] + [dram(f"table{k}", (N_NODES, D)) for k in range(1, PASSES)]
    dst_table = dram("dst_table", (N_NODES, D))
    a_dram = {COUNTS: dram("a_counts", (NPP, P, AROW), BF16), WEIGHTS: dram("a_weights", (NPP, P, AROW))}

    def tiles_of(table, g):
        return table.rearrange("(j q) d -> q j d", q=Q)[:, g * GT:(g + 1) * GT, :]

    with ExitStack() as ctx:
        def sb(name, shape, dt=F32):
            return ctx.enter_context(nc.sbuf_tensor(name, shape, dt))

        def sem(name):
            return ctx.enter_context(nc.semaphore(name))

        stream = sb("stream", [P, 3 * AROW])
        node_room = sb("node_room", [P, 3 * NPP * D])
        SETF = BT * P * 4 // 2 + BT * COLS // 2
        operand_room = sb("operand_room", [P, 2 * SETF])

        def in_room(room, at, n, dt=F32):
            words = n if dt in (F32, I32) else n // 2
            piece = room[:, at:at + words]
            return piece if dt == F32 else piece.bitcast(dt)

        stage = {WEIGHTS: [in_room(stream, b * AROW, AROW) for b in range(2)],
                 COUNTS: [in_room(stream, 2 * AROW + b * AROW // 2, AROW, BF16) for b in range(2)]}
        a_buf = {WEIGHTS: [in_room(stream, b * AROW, AROW) for b in range(3)],
                 COUNTS: [in_room(stream, b * AROW // 2, AROW, BF16) for b in range(GT)]}
        A_SLOT = {WEIGHTS: [0, 1, 2, 0, 1], COUNTS: [0, 1, 2, 3, 4]}
        CH = STEPS * D
        msg = [in_room(stream, s * CH, CH) for s in range(2)]
        frow = in_room(stream, 2 * CH, 2 * CH)
        drow = in_room(stream, 4 * CH, NPP * D).rearrange("p (j d) -> p j d", d=D)
        spill = in_room(stream, 4 * CH + NPP * D, NPP * Q).rearrange("p (j q) -> p j q", q=Q)
        dst_all = in_room(stream, 0, EPP)
        dst_int = in_room(stream, CH, EPP, I32)
        ends = in_room(node_room, 0, NPP * D).rearrange("p (j d) -> p j d", d=D)
        tab1 = in_room(node_room, NPP * D, NPP * D).rearrange("p (j d) -> p j d", d=D)
        keep = in_room(node_room, 2 * NPP * D, NPP * D).rearrange("p (j d) -> p j d", d=D)
        tab0 = ends
        NT = NGROUPS * HALVES
        key_t = in_room(node_room, 0, NT)
        lo_t = in_room(node_room, NT, NT, BF16)
        wp_t = [in_room(node_room, NT + (i + 1) * NT // 2, NT, BF16) for i in range(3)]
        e_tmp = [in_room(node_room, i * EPP, EPP) for i in range(6)]
        onehot = [[in_room(operand_room, b * SETF + i * BT * P // 2, BT * P, BF16)
                   .rearrange("p (t c) -> p t c", c=P) for i in range(4)] for b in range(2)]
        high = [in_room(operand_room, b * SETF + 2 * BT * P, BT * COLS, BF16)
                .rearrange("p (t c) -> p t c", c=COLS) for b in range(2)]
        group_rows = [in_room(operand_room, i * SLOTS, SLOTS) for i in range(6)]
        parts = in_room(operand_room, 0, NPP * 3 * D, BF16).rearrange("p (j c) -> p j c", c=3 * D)

        src_all = sb("src_all", [P, EPP], I32)
        same_all = sb("same_all", [P, EPP])
        w_all = sb("w_all", [P, EPP])
        idx_c = [sb(f"idx_c{s}", [P, STEPS], I32) for s in range(2)]
        same_c = [sb(f"same_c{s}", [P, STEPS]) for s in range(2)]
        w_c = [sb(f"w_c{s}", [P, STEPS]) for s in range(2)]
        state = sb("state", [P, D])
        dstate = sb("dstate", [P, D])
        xcur = sb("xcur", [P, NPP, D])
        total = [sb(f"total{i}", [P, GT, D]) for i in range(2)]
        node_i = sb("node_i", [P, NPP], I32)
        blk_i = sb("blk_i", [P, NPP], I32)
        end_i = sb("end_i", [P, NPP], I32)
        start_i = sb("start_i", [P, NPP], I32)
        node_f, blk_f, cnt, upto, below, deg, has, dinv, norm, norm_has, tmpn, wend = (
            sb(n, [P, NPP]) for n in ("node_f", "blk_f", "cnt", "upto", "below", "deg", "has", "dinv", "norm",
                                      "norm_has", "tmpn", "wend"))
        gstart, gend, gcnt, gbase = (sb(n, [P, GBLK]) for n in ("gstart", "gend", "gcnt", "gbase"))
        gstart_i = sb("gstart_i", [P, GBLK], I32)
        gbase_i = sb("gbase_i", [P, GBLK], I32)
        first_i = sb("first_i", [P, 1], I32)
        next_f, cont, last_f, last_w, eps1, gmax = (
            sb(n, [P, 1]) for n in ("next_f", "cont", "last_f", "last_w", "eps1", "gmax"))
        flag_f = sb("flag_f", [1, 1])
        flag_i = sb("flag_i", [1, 1], I32)
        zeros = sb("zeros", [P, ZROWS * D])
        b0row = sb("b0row", [P, D])
        junk = sb("junk", [P, BLOCKS])
        firsts = in_room(operand_room, 0, BLOCKS)
        firsts_d = in_room(operand_room, BLOCKS, BLOCKS).rearrange("p (b q) -> p b q", q=P)
        ident = sb("ident", [P, P])
        ones = sb("ones", [P, P])
        low_iota = sb("low_iota", [P, P], BF16)
        high_iota = sb("high_iota", [P, 256], F16)
        slot_f = sb("slot_f", [P, SLOTS])
        slot_i = in_room(operand_room, 2 * BLOCKS, SLOTS, I32)
        cat = sb("cat", [P, GT, 2 * D])
        catT = sb("catT", [P, GT, P])
        hidT = sb("hidT", [P, GT, P])
        r = sb("r", [P, GT, D])
        sq = sb("sq", [P, GT, D])
        stat = sb("stat", [P, GT])
        var = sb("var", [P, GT])
        std = sb("std", [P, GT])
        w0 = sb("w0", [D, 2 * D])
        w0T = sb("w0T", [2 * D, D])
        wab = sb("wab", [D, 2 * D])
        w2 = sb("w2", [D, D])
        w3 = sb("w3", [2 * D, HID])
        w3lr = sb("w3lr", [HID, 2 * D])
        b3 = sb("b3", [HID, 1])
        rows = sb("rows", [P, 5, D])
        ROW_B0, ROW_B1, ROW_B2, ROW_B3, ROW_E = range(5)

        ps = ctx.enter_context(nc.psum_tensor("ps", [P, 8 * BANK], F32))

        def bank(b, n=1):
            return ps[:, b * BANK:(b + n) * BANK]

        ps_sum = [bank(b) for b in range(3)]
        ps_spill = [bank(3), bank(2)]
        ps_t = bank(4, 2)
        ps_o = bank(6, 2)
        ps_pack = [bank(b) for b in (5, 6, 7)]
        SUM_BANK = [0, 1, 2, 0, 1]

        filled = sem("filled")
        consts = sem("consts")
        dst_in = sem("dst_in")
        src_in = sem("src_in")
        w_in = sem("w_in")
        e_in = sem("e_in")
        x_in = sem("x_in")
        wts_in = sem("wts_in")
        dst_float = sem("dst_float")
        same_rdy = sem("same_rdy")
        dblk_out = sem("dblk_out")
        next_in = sem("next_in")
        firsts_rdy = sem("firsts_rdy")
        firsts_ps = sem("firsts_ps")
        blk_rdy = sem("blk_rdy")
        blk_row = [sem(f"blk_row{i}") for i in range(RING)]
        blk_used = sem("blk_used")
        pack_rdy = sem("pack_rdy")
        pack_out = sem("pack_out")
        upto_rdy = sem("upto_rdy")
        upto_out = sem("upto_out")
        below_in = sem("below_in")
        end_rdy = sem("end_rdy")
        wend_in = sem("wend_in")
        spill_rdy = sem("spill_rdy")
        wspill = sem("wspill")
        wdeg_rdy = sem("wdeg_rdy")
        norm_root = sem("norm_root")
        gmax_rdy = sem("gmax_rdy")
        gmax_ps = sem("gmax_ps")
        flag_rdy = sem("flag_rdy")
        start_done = sem("start_done")
        w0_ps = sem("w0_ps")
        w0_rdy = sem("w0_rdy")
        zero_out = sem("zero_out")
        group_in = sem("group_in")
        group_rdy = sem("group_rdy")
        group_ps = sem("group_ps")
        group_used = sem("group_used")
        lo_rdy = sem("lo_rdy")
        ops_rdy = sem("ops_rdy")
        pool_rdy = sem("pool_rdy")
        grp_done = sem("grp_done")
        evac = sem("evac")
        stage_out = [sem(f"stage_out{b}") for b in range(2)]
        stage_free = sem("stage_free")
        a_in = [sem(f"a_in{b}") for b in range(GT)]
        dense_done = sem("dense_done")
        dense_used = sem("dense_used")
        parts_rdy = sem("parts_rdy")
        aux_rdy = [sem(f"aux_rdy{k}") for k in range(PASSES)]
        pool_go = sem("pool_go")
        pe_go = sem("pe_go")
        gathered = [[sem(f"gathered{k}_{s}") for s in range(2)] for k in range(PASSES)]
        summed = [sem(f"summed{k}") for k in range(PASSES)]
        stored = [[sem(f"stored{k}_{s}") for s in range(2)] for k in range(PASSES)]
        frow_in = [sem(f"frow_in{s}") for s in range(2)]
        spill_num = sem("spill_num")
        ends_in = [sem(f"ends_in{g}") for g in range(GROUPS)]
        spilled = sem("spilled")
        joined = sem("joined")
        cat_rdy = sem("cat_rdy")
        turned = sem("turned")
        turned_sb = sem("turned_sb")
        hid_ps = sem("hid_ps")
        hid_sb = sem("hid_sb")
        prod = sem("prod")
        prod_used = sem("prod_used")
        prod_tab = sem("prod_tab")
        var_rdy = sem("var_rdy")
        std_rdy = sem("std_rdy")
        tab_rdy = sem("tab_rdy")
        tab_out = sem("tab_out")
        drow_rdy = sem("drow_rdy")
        drow_out = sem("drow_out")
        scattered = sem("scattered")
        b0_in = sem("b0_in")
        b0_out = sem("b0_out")
        out_done = sem("out_done")

        block = ctx.enter_context(nc.Block())

        WITH_CAT = (L0, L1B, L2, L3A)
        WITH_HID = (L3A,)
        WITH_LN = (L0, L1B, L2, L3B)
        TAB_DVE = (L0, L1A, L2, L3B)
        TAB_ACT = (L1B, L3A)
        GATHER = {"linear": (L2,), "gather": (L0, L1A, L1B, L2, L3A, L3B)}
        LINEAR = {m: tuple(k for k in range(PASSES) if k not in GATHER[m]) for m in GATHER}
        TO_DRAM = {m: tuple(k - 1 for k in GATHER[m] if k > 0) for m in GATHER}

        def count(users, k, g):
            return users.index(k) * GROUPS + g + 1

        def before(users, k):
            return sum(u < k for u in users)

        def steps3(tile):
            return tile.rearrange("p (t d) -> p t d", d=D)

        def frow3(s):
            return steps3(frow[:, s * CH:(s + 1) * CH])

        def ps3(p, w, n=GT):
            return p[0:Q, 0:n * w].rearrange("p (j d) -> p j d", d=w)

        def per_node(col, g, w=D):
            return col[0:Q, g * GT:(g + 1) * GT].unsqueeze(2).to_broadcast([Q, GT, w])

        def row_bc(i, n=GT):
            return rows[0:Q, i:i + 1, :].to_broadcast([Q, n, D])

        def grp(tile, g):
            return tile[0:Q, g * GT:(g + 1) * GT, :]

        def tab_out_of(k, mode):
            return tab0 if k == L1A and mode == "linear" else tab1

        def tab_in_of(k):
            return {L1A: tab1, L1B: tab0}[k]

        def both(eng, run):
            eng.wait_ge(flag_rdy, 1)
            fits = eng.value_load(flag_i[0:1, 0:1], min_val=0, max_val=1)
            with eng.If(fits):
                run("linear")
            with eng.Else():
                run("gather")
            eng.drain()

        @block.sync
        def _(sp):
            def load_edges(tile, flat, signal):
                main = flat[0:(P - 1) * EPP].rearrange("(p t) -> p t", p=P - 1)
                sp.dma_start(tile[0:P - 1, :], main).then_inc(signal, 16)
                last = flat[(P - 1) * EPP:N_EDGES].rearrange("(p t) -> p t", p=1)
                sp.dma_start(tile[P - 1:P, 0:TAIL], last).then_inc(signal, 16)

            sp.wait_ge(filled, 1)
            load_edges(dst_int, dst, dst_in)
            sp.wait_ge(filled, 3)
            load_edges(w_all, edge_w, w_in)
            load_edges(src_all, src, src_in)
            sp.dma_start(xcur[0:Q, :, :], x.rearrange("(j q) d -> q j d", q=Q)).then_inc(x_in, 16)
            sp.wait_ge(dst_float, 1)
            sp.dma_start(dst_blocks.rearrange("(p b) t -> p (b t)", p=P), dst_all[:, :]).then_inc(dblk_out, 16)
            sp.wait_ge(filled, 5)
            sp.dma_start(next_f[0:P - 1, :], dst_all[1:P, 0:1]).then_inc(next_in, 16)
            sp.wait_ge(pack_rdy, 1)
            for i, tile in enumerate((e_tmp[0], e_tmp[1], w_all)):
                sp.dma_start(packed[i][0:EDGES, :].rearrange("(p t) a -> p (t a)", p=P), tile[:, :])\
                  .then_inc(pack_out, 16)
                sp.dma_start(packed[i][EDGES:EDGES + SLOTS, :].rearrange("(p t) a -> p (t a)", p=1),
                             zeros[0:1, 0:SLOTS]).then_inc(pack_out, 16)
            sp.dma_start(running_w.rearrange("(p t) a -> p (t a)", p=P), e_tmp[2][:, :]).then_inc(pack_out, 16)
            sp.wait_ge(upto_rdy, 1)
            sp.dma_start(edges_upto[1:N_NODES + 1].rearrange("(j q) -> q j", q=Q), upto[0:Q, :],
                         allow_slow_non_contiguous=True).then_inc(upto_out, 16)
            sp.dma_start(edges_upto[0:1].rearrange("(p j) -> p j", p=1), zeros[0:1, 0:1]).then_inc(upto_out, 16)
            sp.wait_ge(upto_out, 32)
            sp.dma_start(below[0:Q, :], edges_upto[0:N_NODES].rearrange("(j q) -> q j", q=Q),
                         allow_slow_non_contiguous=True).then_inc(below_in, 16)
            for tile, at in ((gstart, 0), (gend, GNODES)):
                groups = edges_upto[at:at + N_NODES].rearrange("(b q r) -> q b r", q=Q, r=GNODES)
                sp.dma_start(tile[0:Q, :], groups[:, :, 0], allow_slow_non_contiguous=True).then_inc(below_in, 16)

            flat_first = first_rows[0:EDGES, :].rearrange("(p t) d -> p (t d)", p=P)

            def zero_first(n):
                sp.dma_start(flat_first[:, bass.ds(n * (ZROWS * D), ZROWS * D)], zeros[:, :]).then_inc(zero_out, 16)

            def store_matrices():
                with sp.Fori(0, TURNS) as i:
                    for b in range(2):
                        sp.wait_ge(evac, i * ITG + (BUILD_BANKS + (b + 1) * GPB))
                        for what in (WEIGHTS, COUNTS):
                            to = a_dram[what].rearrange("j p c -> p j c")[:, bass.ds(i * 2 + b, 1), :]
                            sp.dma_start(to, stage[what][b][:, :].unsqueeze(1)).then_inc(stage_out[b], 16)
                        zero_first(i * 2 + b)
                    for b in range(2):
                        sp.wait_ge(stage_out[b], (i + 1) * 32)
                        sp.sem_inc(stage_free, 1)
                with sp.Fori(2 * TURNS, ZSTORES) as n:
                    zero_first(n)

            def load_a(k, g, first=False):
                what = MATRIX[k]
                base = before(LINEAR["linear"], k) * NPP
                for b in range(GT):
                    if what == WEIGHTS and b >= 3:
                        sp.wait_ge(dense_done, g * GT + (base + b - 2))
                    elif not first:
                        last = {WEIGHTS: (3, 4, 2, 3, 4), COUNTS: range(GT)}[what][b]
                        sp.wait_ge(dense_done, g * GT + (base + last + 1 - GT))
                    sp.dma_start(a_buf[what][A_SLOT[what][b]][:, :].unsqueeze(1),
                                 a_dram[what].rearrange("j p c -> p j c")[:, bass.ds(g * GT + b, 1), :])\
                      .then_inc(a_in[b], 16)

            def store(k, s, pair):
                rows_of = running.rearrange("(p t) d -> p (t d)", p=P)
                sp.wait_ge(summed[k], 2 * pair + s + 1)
                sp.dma_start(rows_of[:, bass.ds((2 * pair + s) * CH, CH)], msg[s][:, :]).then_inc(stored[k][s], 16)

            def load_first(s, pair):
                sp.dma_start(frow[:, s * CH:(s + 1) * CH],
                             flat_first[:, bass.ds((2 * pair + s) * CH, CH)]).then_inc(frow_in[s], 16)

            def store_nodes(k, g, mode):
                if k in TO_DRAM[mode]:
                    if k in TAB_DVE:
                        sp.wait_ge(tab_rdy, count(TAB_DVE, k, g))
                    else:
                        sp.wait_ge(prod_tab, count(TAB_ACT, k, g))
                    source = xcur if k == L2 else tab_out_of(k, mode)
                    sp.dma_start(tiles_of(tables[k + 1], g), grp(source, g)).then_inc(tab_out, 16)
                if k == L1B:
                    sp.wait_ge(drow_rdy, g + 1)
                    sp.dma_start(tiles_of(dst_table, g), grp(drow, g)).then_inc(drow_out, 16)
                if k == L3B:
                    sp.wait_ge(tab_rdy, count(TAB_DVE, k, g))
                    sp.dma_start(tiles_of(out, g), grp(xcur, g)).then_inc(out_done, 16)

            def run(mode):
                if mode == "linear":
                    store_matrices()
                else:
                    with sp.Fori(0, ZSTORES) as n:
                        zero_first(n)
                for k in range(PASSES):
                    if k in GATHER[mode]:
                        if k == L2:
                            load_edges(w_all, edge_e, e_in)
                            sp.wait_ge(scattered, 16 * NPP)
                            sp.wait_ge(b0_in, 16)
                            sp.dma_start(steps3(flat_first)[:, 0, :], b0row[:, :]).then_inc(b0_out, 16)
                            sp.wait_ge(b0_out, 16)
                            load_first(0, 0)
                            load_first(1, 0)
                        with sp.Fori(0, PAIRS - 1) as pair:
                            for s in range(2):
                                store(k, s, pair)
                                if k == L2:
                                    load_first(s, pair + 1)
                        for s in range(2):
                            store(k, s, PAIRS - 1)
                        for g in range(GROUPS):
                            store_nodes(k, g, mode)
                    else:
                        if before(LINEAR[mode], k):
                            sp.wait_ge(dense_done, before(LINEAR[mode], k) * NPP)
                        if k == L3A:
                            sp.wait_ge(joined, GROUPS)
                        load_a(k, 0, first=True)
                        if k in (L1B, L3B):
                            for g in range(1, GROUPS):
                                load_a(k, g)
                                if k == L3B:
                                    store_nodes(k, g - 1, mode)
                            if k == L1B:
                                for g in range(GROUPS):
                                    store_nodes(k, g, mode)
                            else:
                                store_nodes(k, GROUPS - 1, mode)
                        else:
                            with sp.Fori(1, GROUPS) as g:
                                load_a(k, g)
                sp.wait_ge(out_done, 16 * GROUPS)
                sp.wait_ge(zero_out, 16 * ZSTORES)

            both(sp, run)

        @block.gpsimd
        def _(pool):
            def numbers(tile, pattern):
                return pool.iota(tile, pattern=pattern, base=0, channel_multiplier=0)

            pool.memset(dst_int[:, :], int(NO_NODE)).then_inc(filled, 1)
            pool.memset(src_all[:, :], 0).then_inc(filled, 1)
            pool.memset(w_all[:, :], 0.0).then_inc(filled, 1)
            pool.memset(zeros[:, :], 0.0).then_inc(filled, 1)
            pool.memset(next_f[:, :], -1.0).then_inc(filled, 1)
            pool.memset(ident[:, :], 0.0).then_inc(consts, 1)
            pool.memset(ones[:, :], 1.0).then_inc(consts, 1)
            pool.memset(eps1[:, :], EPS).then_inc(consts, 1)
            pool.iota(node_i[:, :], pattern=[[Q, NPP]], base=0, channel_multiplier=1).then_inc(consts, 1)
            pool.iota(gbase_i[:, :], pattern=[[GNODES * Q, GBLK]], base=0, channel_multiplier=GNODES)\
                .then_inc(consts, 1)
            numbers(slot_i[:, :], [[1, SLOTS]]).then_inc(consts, 1)
            pool.wait_ge(consts, 6)
            pool.affine_select(out=ident[:, :], in_=ident[:, :], compare_op=ALU.not_equal, fill=1.0, base=0,
                               pattern=[[-1, P]], channel_multiplier=1).then_inc(consts, 1)
            numbers(spill.bitcast(I32), [[Q, NPP], [1, Q]]).then_inc(spill_num, 1)

            pool.wait_ge(dblk_out, 16)
            pool.wait_ge(blk_rdy, 1)
            for j in range(NPP):
                if j >= RING:
                    pool.wait_ge(blk_used, j - RING + 1)
                pool.indirect_dma_start(frow[0:Q, (j % RING) * BLK:(j % RING + 1) * BLK], None, dst_blocks[:, :],
                                        bass.IndirectOffsetOnAxis(blk_i[0:Q, j:j + 1], 0))\
                    .then_inc(blk_row[j % RING], 16)
            pool.wait_ge(pack_out, 16 * 7)
            pool.wait_ge(end_rdy, 1)
            for j in range(NPP):
                pool.indirect_dma_start(wend[0:Q, j:j + 1], None, running_w[:, :],
                                        bass.IndirectOffsetOnAxis(end_i[0:Q, j:j + 1], 0)).then_inc(wend_in, 16)

            def gather_groups():
                for b in range(GBLK):
                    if b >= 2:
                        pool.wait_ge(group_ps, b - 1)
                    for i in range(3):
                        pool.indirect_dma_start(group_rows[(b % 2) * 3 + i][0:Q, :], None, packed[i][:, :],
                                                bass.IndirectOffsetOnAxis(gstart_i[0:Q, b:b + 1], 0))\
                            .then_inc(group_in, 16)
                    pool.wait_ge(group_in, 48 * (b + 1))

            def build_part():
                with pool.Fori(0, TURNS) as i:
                    for bt in range(ITB):
                        pool.wait_ge(lo_rdy, i * ITB + (bt + 1))
                        pool.sem_inc(pool_go, 1)
                        for part in (1, 2):
                            wp = wp_t[part][:, bass.ds(i * (ITB * BT) + bt * BT, BT)]
                            pool.tensor_tensor(onehot[bt % 2][part + 1], onehot[bt % 2][0],
                                               wp.unsqueeze(2).to_broadcast([P, BT, P]), ALU.mult)\
                                .then_inc(pool_rdy, 1)

            def gather_chunk(k, s):
                for t in range(STEPS):
                    pool.indirect_dma_start(steps3(msg[s])[:, t, :], None, tables[k][:, :],
                                            bass.IndirectOffsetOnAxis(idx_c[s][:, t:t + 1], 0))\
                        .then_inc(gathered[k][s], 16)

            def run(mode):
                if mode == "linear":
                    gather_groups()
                    build_part()
                for k in GATHER[mode]:
                    if k > 0:
                        pool.wait_ge(tab_out, 16 * GROUPS * (TO_DRAM[mode].index(k - 1) + 1))
                    if k == L2:
                        pool.wait_ge(zero_out, 16 * ZSTORES)
                        for j in range(NPP):
                            if j % GT == 0:
                                pool.wait_ge(drow_rdy, j // GT + 1)
                            pool.indirect_dma_start(first_rows[:, :],
                                                    bass.IndirectOffsetOnAxis(start_i[0:Q, j:j + 1], 0),
                                                    drow[0:Q, j, :], None).then_inc(scattered, 16)
                        pool.wait_ge(drow_out, 16 * GROUPS)
                        pool.indirect_dma_start(b0row[:, :], None, dst_table[:, :],
                                                bass.IndirectOffsetOnAxis(first_i[:, 0:1], 0)).then_inc(b0_in, 16)
                        if mode == "linear":
                            numbers(spill.bitcast(I32), [[Q, NPP], [1, Q]]).then_inc(spill_num, 1)
                    for s in range(2):
                        pool.wait_ge(aux_rdy[k], s + 1)
                        gather_chunk(k, s)
                    with pool.Fori(0, PAIRS - 1) as pair:
                        for s in range(2):
                            pool.wait_ge(stored[k][s], (pair + 1) * 16)
                            pool.wait_ge(aux_rdy[k], pair * 2 + (s + 3))
                            pool.sem_inc(pool_go, 1)
                            gather_chunk(k, s)
                    for s in range(2):
                        pool.wait_ge(stored[k][s], 16 * PAIRS)
                    if GATHER[mode].index(k):
                        pool.wait_ge(joined, GATHER[mode].index(k) * GROUPS)
                    for j in range(NPP):
                        pool.indirect_dma_start(ends[0:Q, j, :], None, running[:, :],
                                                bass.IndirectOffsetOnAxis(end_i[0:Q, j:j + 1], 0))\
                            .then_inc(ends_in[j // GT], 16)

            both(pool, run)

        @block.scalar
        def _(act):
            act.dma_start(w0[:, :], L0_W).then_inc(wts_in, 16)
            act.dma_start(wab[:, 0:D], L2_W1[0:D, :]).then_inc(wts_in, 16)
            act.dma_start(wab[:, D:2 * D], L2_W1[D:2 * D, :]).then_inc(wts_in, 16)
            act.dma_start(w2[:, :], L2_W2).then_inc(wts_in, 16)
            act.dma_start(w3[0:D, :], L3_W1_l).then_inc(wts_in, 16)
            act.dma_start(w3[D:2 * D, :], L3_W1_r).then_inc(wts_in, 16)
            act.dma_start(w3lr[:, 0:D], L3_W2_l).then_inc(wts_in, 16)
            act.dma_start(w3lr[:, D:2 * D], L3_W2_r).then_inc(wts_in, 16)
            act.dma_start(b3[:, :], L3_b1.rearrange("(p a) -> p a", a=1)).then_inc(wts_in, 16)
            for i, b in ((ROW_B0, L0_b), (ROW_B1, L2_b1), (ROW_B2, L2_b2), (ROW_B3, L3_b2)):
                act.dma_start(rows[:, i, :], b.partition_broadcast(P)).then_inc(wts_in, 16)
            act.dma_start(rows[:, ROW_E, :], L2_W1[2 * D, :].partition_broadcast(P)).then_inc(wts_in, 16)
            act.wait_ge(w0_ps, 1)
            act.copy(w0T[:, :], ps_t[:, 0:D]).then_inc(w0_rdy, 1)
            act.wait_ge(wdeg_rdy, 1)
            act.activation(norm[0:Q, :], tmpn[0:Q, :], ACT.Sqrt).then_inc(norm_root, 1)

            def copy_out():
                act.sem_inc(evac, BUILD_BANKS)
                act.sem_inc(stage_free, 2)
                with act.Fori(0, TURNS) as i:
                    for gi in range(ITG):
                        b, at = gi // GPB, (gi % GPB) * GNODES
                        if gi % GPB == 0:
                            act.wait_ge(stage_free, i * 2 + (b + 1))
                        act.wait_ge(grp_done, i * ITG + (2 * BATCH + gi + 1))
                        for what, col in ((COUNTS, 0), (WEIGHTS, 256)):
                            place = stage[what][b].rearrange("p (h q) -> p h q", q=Q)[:, :, at:at + GNODES]
                            psum = bank(gi % BUILD_BANKS)[:, col:col + COLS].rearrange("p (h r) -> p h r", r=GNODES)
                            ins = act.copy(place, psum)
                        ins.then_inc(evac, 1)

            def aux(k, s, pair):
                at = bass.ds((2 * pair + s) * STEPS, STEPS)
                if k in (L1A, L1B, L2):
                    act.copy(w_c[s][:, :], w_all[:, at])
                act.copy(same_c[s][:, :], same_all[:, at])
                act.copy(idx_c[s][:, :], src_all[:, at])
                act.drain()
                act.sem_inc(aux_rdy[k], 1)

            def root(k, g):
                act.wait_ge(var_rdy, count(WITH_LN, k, g))
                act.activation(std[0:Q, :], var[0:Q, :], ACT.Sqrt, bias=eps1[0:Q, :], scale=1.0 / D)\
                   .then_inc(std_rdy, 1)

            def nodes(k, g, mode):
                if k == L1B:
                    root(k, g)
                if k in WITH_CAT:
                    kr = D if k in (L1B, L2) else 2 * D
                    act.wait_ge(turned, count(WITH_CAT, k, g))
                    if (k, g) != (WITH_CAT[0], 0):
                        act.wait_ge(prod, count(WITH_CAT, k, g) - 1)
                    act.copy(catT[0:kr, :, 0:Q], ps_t[0:kr, 0:GT * P].rearrange("p (j c) -> p j c", c=P)[:, :, 0:Q])\
                       .then_inc(turned_sb, 1)
                if k in WITH_HID:
                    act.wait_ge(hid_ps, count(WITH_HID, k, g))
                    act.activation(hidT[:, :, 0:Q], ps_t[:, 0:GT * P].rearrange("p (j c) -> p j c", c=P)[:, :, 0:Q],
                                   ACT.Relu, bias=b3[:, :]).then_inc(hid_sb, 1)
                if k in TAB_ACT:
                    act.wait_ge(prod, count(WITH_CAT, k, g))
                    act.copy(grp(tab1, g), ps3(ps_o, 2 * D)[:, :, 0:D]).then_inc(prod_tab, 1)
                if k in (L0, L2, L3B):
                    root(k, g)

            def run(mode):
                if mode == "linear":
                    copy_out()
                for k in range(PASSES):
                    if k in GATHER[mode]:
                        if GATHER[mode].index(k):
                            act.wait_ge(summed[k - 1], CHUNKS)
                        if k == L2:
                            act.wait_ge(e_in, 32)
                        aux(k, 0, 0)
                        aux(k, 1, 0)
                        with act.Fori(0, PAIRS - 1) as pair:
                            for s in range(2):
                                act.wait_ge(summed[k], pair * 2 + (s + 1))
                                aux(k, s, pair + 1)
                    for g in range(GROUPS):
                        nodes(k, g, mode)

            act.wait_ge(src_in, 32)
            both(act, run)

        @block.tensor
        def _(pe):
            pe.wait_ge(firsts_rdy, 1)
            pe.matmul(ps_o[:, 0:BLOCKS], ones[:, :], firsts_d[:, :, :].rearrange("p b q -> p (b q)"),
                      start=True, stop=True).then_inc(firsts_ps, 1)
            pe.wait_ge(wts_in, 14 * 16)
            pe.transpose(ps_t[:, 0:D], w0[:, :], ident[0:D, 0:D]).then_inc(w0_ps, 1)
            pe.wait_ge(spill_rdy, 1)
            for j in range(NPP):
                ins = pe.matmul(bank(3)[0:Q, j:j + 1], spill[:, j, :], last_w[:, :], start=True, stop=True)
            ins.then_inc(wspill, 1)
            pe.wait_ge(gmax_rdy, 1)
            pe.transpose(bank(2)[0:1, 0:Q], gmax[0:Q, :], ident[0:Q, 0:Q]).then_inc(gmax_ps, 1)
            pe.wait_ge(w0_rdy, 1)

            def turn_groups():
                for b in range(GBLK):
                    pe.wait_ge(group_rdy, b + 1)
                    if b:
                        pe.wait_ge(group_used, b)
                    for i in range(3):
                        for h in range(HALVES):
                            ins = pe.transpose(ps_pack[i][:, h * Q:(h + 1) * Q],
                                               group_rows[(b % 2) * 3 + i][0:Q, h * P:(h + 1) * P], ident[0:Q, 0:Q])
                    ins.then_inc(group_ps, 1)

            def build():
                pe.sem_inc(grp_done, 2 * BATCH)
                with pe.Fori(0, TURNS) as i:
                    for gi in range(ITG):
                        bt, s = gi // BATCH, (gi // BATCH) % 2
                        if gi % BATCH == 0:
                            pe.wait_ge(ops_rdy, i * ITB + (bt + 1))
                            pe.wait_ge(pool_rdy, i * (2 * ITB) + 2 * (bt + 1))
                        pe.wait_ge(evac, i * ITG + (gi + 1))
                        out_bank = bank(gi % BUILD_BANKS)
                        tiles = [(gi % BATCH) * HALVES + h for h in range(HALVES)]
                        for t in tiles:
                            pe.matmul(out_bank[:, 0:COLS], onehot[s][0][:, t, :], high[s][:, t, :],
                                      start=t == tiles[0], stop=t == tiles[-1])
                        for t in tiles:
                            for part in range(3):
                                ins = pe.matmul(out_bank[:, 256:256 + COLS], onehot[s][1 + part][:, t, :],
                                                high[s][:, t, :], start=(t, part) == (tiles[0], 0),
                                                stop=(t, part) == (tiles[-1], 2))
                        ins.then_inc(grp_done, 1)

            def dense(k, g):
                what = MATRIX[k]
                lin = before(LINEAR["linear"], k)
                for b in range(GT):
                    pe.wait_ge(a_in[b], g * 16 + (lin * GROUPS + 1) * 16)
                    used = lin * NPP + b + (-2 if b >= 3 else (3, 4, 2)[b] - b - GT + 1)
                    if isinstance(g, int) and g == 0 and used <= 0:
                        pass
                    else:
                        pe.wait_ge(dense_used, g * GT + used)
                    a = a_buf[what][A_SLOT[what][b]].rearrange("p (h q) -> p h q", q=Q)
                    for h in range(NPP):
                        if what == COUNTS:
                            ins = pe.matmul(ps_sum[SUM_BANK[b]][0:Q, 0:3 * D], a[0:Q, h, :], parts[0:Q, h, :],
                                            start=h == 0, stop=h == NPP - 1)
                        else:
                            ins = pe.matmul(ps_sum[SUM_BANK[b]][0:Q, 0:D], a[0:Q, h, :], tab_in_of(k)[0:Q, h, :],
                                            start=h == 0, stop=h == NPP - 1)
                    ins.then_inc(dense_done, 1)

            def carry(k, g, mode):
                n = GATHER[mode].index(k) * GROUPS + g
                pe.wait_ge(summed[k], CHUNKS)
                if k == L2 and mode == "linear":
                    pe.wait_ge(spill_rdy, 2)
                if n >= 2:
                    pe.wait_ge(joined, n - 1)
                for j in range(GT):
                    ins = pe.matmul(ps_spill[n % 2][0:Q, j * D:(j + 1) * D], spill[:, g * GT + j, :], state[:, :],
                                    start=True, stop=True)
                ins.then_inc(spilled, 1)

            def nodes(k, g):
                if k not in WITH_CAT:
                    return
                done = g + WITH_CAT.index(k) * GROUPS
                first = isinstance(g, int) and done == 0
                kr = D if k in (L1B, L2) else 2 * D
                pe.wait_ge(cat_rdy, done + 1)
                if not first:
                    pe.wait_ge(turned_sb, done)
                pe.sem_inc(pe_go, 1)
                for j in range(GT):
                    ins = pe.transpose(ps_t[0:kr, j * P:j * P + Q], cat[0:Q, j, 0:kr], ident[0:Q, 0:Q])
                ins.then_inc(turned, 1)
                pe.wait_ge(turned_sb, done + 1)
                if k in WITH_HID:
                    ps_tt = ps_t[:, 0:GT * P].rearrange("p (j c) -> p j c", c=P)
                    for lo, hi in ((0, 4), (4, GT)):
                        ins = pe.matmul(ps_tt[:, lo:hi, 0:Q], w3[:, :], catT[:, lo:hi, 0:Q], start=True, stop=True)
                    ins.then_inc(hid_ps, 1)
                    pe.wait_ge(hid_sb, g + 1)
                if not first:
                    pe.wait_ge(prod_used, done)
                for j in range(GT):
                    if k == L0:
                        ins = pe.matmul(ps_o[0:Q, j * D:(j + 1) * D], catT[:, j, 0:Q], w0T[:, :],
                                        start=True, stop=True)
                    elif k == L1B:
                        ins = pe.matmul(ps_o[0:Q, j * P:(j + 1) * P], catT[0:D, j, 0:Q], wab[:, :],
                                        start=True, stop=True)
                    elif k == L2:
                        ins = pe.matmul(ps_o[0:Q, j * D:(j + 1) * D], catT[0:D, j, 0:Q], w2[:, :],
                                        start=True, stop=True)
                    else:
                        ins = pe.matmul(ps_o[0:Q, j * P:(j + 1) * P], hidT[:, j, 0:Q], w3lr[:, :],
                                        start=True, stop=True)
                ins.then_inc(prod, 1)

            def run(mode):
                if mode == "linear":
                    turn_groups()
                    build()
                for k in range(PASSES):
                    if k in GATHER[mode]:
                        carry(k, 0, mode)
                        carry(k, 1, mode)
                        for g in range(GROUPS):
                            nodes(k, g)
                            if g + 2 < GROUPS:
                                carry(k, g + 2, mode)
                    else:
                        if MATRIX[k] == COUNTS:
                            pe.wait_ge(parts_rdy, (L0, L3A, L3B).index(k) + 1)
                        else:
                            pe.wait_ge(tab_rdy, (TAB_DVE.index(k - 1) + 1) * GROUPS)
                        dense(k, 0)
                        nodes(k, 0)
                        with pe.Fori(1, GROUPS) as g:
                            dense(k, g)
                            nodes(k, g)

            both(pe, run)

        @block.vector
        def _(v):
            v.wait_ge(dst_in, 32)
            v.tensor_copy(dst_all[:, :], dst_int[:, :]).then_inc(dst_float, 1)
            v.memset(same_all[:, 0:1], 0.0)
            v.drain()
            v.tensor_tensor(same_all[:, 1:EPP], dst_all[:, 1:EPP], dst_all[:, 0:EPP - 1], ALU.is_equal)
            v.wait_ge(consts, 7)
            for b in range(BPP):
                v.tensor_scalar(firsts_d[:, b, :], ident[:, :], dst_all[:, b * BLK:b * BLK + 1], None, ALU.mult)
            v.tensor_copy(node_f[:, :], node_i[:, :])
            v.tensor_copy(first_i[:, :], dst_all[:, 0:1])
            v.tensor_copy(last_f[:, :], dst_all[:, EPP - 1:EPP])
            v.tensor_copy(slot_f[:, :], slot_i[:, :])
            v.tensor_copy(low_iota[:, :], slot_i[:, 0:P])
            v.tensor_copy(high_iota[:, :], slot_i[:, 0:256])
            v.tensor_copy(gbase[:, :], gbase_i[:, :])
            v.drain()
            v.sem_inc(firsts_rdy, 1)
            v.wait_ge(firsts_ps, 1)
            v.tensor_copy(firsts[:, :], ps_o[:, 0:BLOCKS])
            v.drain()
            for j in range(NPP):
                v.tensor_scalar(junk[:, 0:BLOCKS], firsts[:, :], node_f[:, j:j + 1], None, ALU.is_le, ALU.add,
                                accum_out=cnt[:, j:j + 1])
                v.drain()
            v.tensor_scalar(blk_f[:, :], cnt[:, :], -1.0, 0.0, ALU.add, ALU.max)
            v.drain()
            v.tensor_copy(blk_i[:, :], blk_f[:, :]).then_inc(blk_rdy, 1)
            hd, lo, run_w, hi, off, fsrc = e_tmp
            hi_int = off.bitcast(I32)
            v.wait_ge(src_in, 32)
            v.tensor_copy(fsrc, src_all[:, :])
            v.drain()
            v.tensor_scalar(hi, fsrc, 1.0 / Q, None, ALU.mult)
            v.drain()
            v.tensor_copy(hi_int, hi)
            v.drain()
            v.tensor_copy(hi, hi_int)
            v.drain()
            v.scalar_tensor_tensor(lo, hi, -float(Q), fsrc, ALU.mult, ALU.add)
            v.drain()
            v.tensor_scalar(off, lo, 0.0, None, ALU.is_lt)
            v.tensor_scalar(hd, lo, float(Q), None, ALU.is_ge)
            v.drain()
            v.tensor_tensor(off, hd, off, ALU.subtract)
            v.drain()
            v.tensor_tensor(hi, hi, off, ALU.add)
            v.scalar_tensor_tensor(lo, off, -float(Q), lo, ALU.mult, ALU.add)
            v.drain()
            v.scalar_tensor_tensor(hd, hi, float(GNODES), dst_all[:, :], ALU.mult, ALU.add)
            v.wait_ge(w_in, 32)
            v.tensor_tensor_scan(run_w, same_all[:, :], w_all[:, :], 0.0, ALU.mult, ALU.add)
            v.drain()
            v.tensor_copy(last_w[:, :], run_w[:, EPP - 1:EPP])
            v.drain()
            v.wait_ge(filled, 4)
            v.sem_inc(pack_rdy, 1)
            v.wait_ge(next_in, 16)
            v.tensor_tensor(cont[:, :], next_f[:, :], last_f[:, :], ALU.is_equal)
            v.drain()

            def fill_spill(n):
                v.wait_ge(spill_num, n)
                v.tensor_scalar(spill, spill.bitcast(I32), last_f[:, :], cont[:, 0:1], ALU.is_equal, ALU.mult)\
                 .then_inc(spill_rdy, 1)

            fill_spill(1)
            for j in range(NPP):
                v.wait_ge(blk_row[j % RING], 16 * (j // RING + 1))
                v.tensor_scalar(junk[0:Q, 0:BLK], frow[0:Q, (j % RING) * BLK:(j % RING + 1) * BLK],
                                node_f[0:Q, j:j + 1], None, ALU.is_le, ALU.add, accum_out=cnt[0:Q, j:j + 1])\
                 .then_inc(blk_used, 1)
                v.drain()

            def n(tile):
                return tile[0:Q, :]

            v.scalar_tensor_tensor(n(upto), n(blk_f), float(BLK), n(cnt), ALU.mult, ALU.add).then_inc(upto_rdy, 1)
            v.drain()
            v.tensor_scalar(n(tmpn), n(upto), -1.0, 0.0, ALU.add, ALU.max)
            v.drain()
            v.tensor_copy(n(end_i), n(tmpn)).then_inc(end_rdy, 1)
            v.wait_ge(below_in, 48)
            v.tensor_tensor(n(deg), n(upto), n(below), ALU.subtract)
            v.tensor_tensor(n(gcnt), n(gend), n(gstart), ALU.subtract)
            v.tensor_copy(n(gstart_i), n(gstart))
            v.drain()
            v.tensor_reduce(n(gmax), n(gcnt), AX.X, ALU.max).then_inc(gmax_rdy, 1)
            v.tensor_scalar(n(has), n(deg), 1.0, None, ALU.min)
            v.tensor_scalar(n(dinv), n(deg), 1.0, None, ALU.max)
            v.tensor_scalar(n(cnt), n(node_f), float(EDGES), None, ALU.add)
            v.drain()
            v.reciprocal(n(dinv), n(dinv))
            v.tensor_tensor(n(below), n(below), n(cnt), ALU.subtract)
            v.drain()
            v.tensor_tensor(n(dinv), n(dinv), n(has), ALU.mult)
            v.tensor_tensor(n(below), n(below), n(has), ALU.mult)
            v.drain()
            v.tensor_tensor(n(below), n(below), n(cnt), ALU.add)
            v.drain()
            v.tensor_copy(n(start_i), n(below))
            v.wait_ge(gmax_ps, 1)
            v.tensor_reduce(flag_f[:, :], bank(2)[0:1, 0:Q], AX.X, ALU.max)
            v.drain()
            v.tensor_scalar(flag_f[:, :], flag_f[:, :], float(MAX_GROUP), None, ALU.is_le)
            v.drain()
            v.tensor_copy(flag_i[:, :], flag_f[:, :])
            v.wait_ge(wend_in, 16 * NPP)
            v.wait_ge(wspill, 1)
            v.tensor_tensor(n(wend), n(wend), bank(3)[0:Q, 0:NPP], ALU.add)
            v.drain()
            v.tensor_tensor(n(wend), n(wend), n(has), ALU.mult)
            v.drain()
            v.tensor_scalar(n(tmpn), n(wend), 1.0, None, ALU.max).then_inc(wdeg_rdy, 1)
            v.wait_ge(norm_root, 1)
            v.reciprocal(n(norm), n(norm))
            v.drain()
            v.tensor_tensor(n(norm_has), n(norm), n(has), ALU.mult)
            v.wait_ge(pack_out, 16 * 7)
            v.wait_ge(x_in, 16)
            v.wait_ge(wts_in, 14 * 16)
            v.drain()
            v.sem_inc(flag_rdy, 1)

            def keys():
                def t3(tile, b, h=None):
                    piece = tile.rearrange("p (g h) -> p g h", h=HALVES)[:, b * Q:(b + 1) * Q, :]
                    return piece.rearrange("p g h -> p h g")

                for b in range(GBLK):
                    key, low, weight = group_rows[(b % 2) * 3:(b % 2) * 3 + 3]
                    v.wait_ge(group_in, 48 * (b + 1))
                    v.tensor_scalar(junk[0:Q, 0:SLOTS], slot_f[0:Q, :], gcnt[0:Q, b:b + 1], FAR, ALU.is_ge, ALU.mult)
                    v.drain()
                    v.scalar_tensor_tensor(key[0:Q, :], key[0:Q, :], gbase[0:Q, b:b + 1], junk[0:Q, 0:SLOTS],
                                           ALU.subtract, ALU.add)
                    v.drain()
                    v.sem_inc(group_rdy, 1)
                    v.wait_ge(group_ps, b + 1)
                    p3 = [p[:, 0:HALVES * Q].rearrange("p (h g) -> p h g", g=Q) for p in ps_pack]
                    rest = junk[:, 0:HALVES * Q].rearrange("p (h g) -> p h g", g=Q)
                    v.tensor_copy(t3(key_t, b), p3[0])
                    v.tensor_copy(t3(lo_t, b), p3[1])
                    v.tensor_copy(t3(wp_t[0], b), p3[2])
                    v.drain()
                    v.tensor_tensor(rest, p3[2], t3(wp_t[0], b), ALU.subtract)
                    v.drain()
                    v.sem_inc(group_used, 1)
                    v.tensor_copy(t3(wp_t[1], b), rest)
                    v.drain()
                    v.tensor_tensor(rest, rest, t3(wp_t[1], b), ALU.subtract)
                    v.drain()
                    v.tensor_copy(t3(wp_t[2], b), rest)
                    v.drain()

            def one_hot():
                with v.Fori(0, TURNS) as i:
                    for bt in range(ITB):
                        s, at = bt % 2, bass.ds(i * (ITB * BT) + bt * BT, BT)
                        v.wait_ge(grp_done, i * ITG + (bt + 1) * BATCH)
                        v.tensor_tensor(onehot[s][0], low_iota[:, :].unsqueeze(1).to_broadcast([P, BT, P]),
                                        lo_t[:, at].unsqueeze(2).to_broadcast([P, BT, P]), ALU.is_equal)\
                         .then_inc(lo_rdy, 1)
                        for t in range(BT):
                            col = bass.ds(i * (ITB * BT) + (bt * BT + t), 1)
                            v.tensor_scalar(high[s][:, t, :], high_iota[:, 0:COLS], key_t[:, col], None,
                                            ALU.is_equal)
                        v.drain()
                        v.tensor_tensor(onehot[s][1], onehot[s][0],
                                        wp_t[0][:, at].unsqueeze(2).to_broadcast([P, BT, P]), ALU.mult)
                        v.drain()
                        v.sem_inc(ops_rdy, 1)

            def split(tile, lo, hi):
                for a in range(lo, hi, GT):
                    x_in3 = tile[0:Q, a:a + GT, :]
                    piece = [parts[0:Q, a:a + GT, i * D:(i + 1) * D] for i in range(3)]
                    v.tensor_copy(piece[0], x_in3)
                    v.drain()
                    v.tensor_tensor(sq[0:Q], x_in3, piece[0], ALU.subtract)
                    v.drain()
                    v.tensor_copy(piece[1], sq[0:Q])
                    v.drain()
                    v.tensor_tensor(sq[0:Q], sq[0:Q], piece[1], ALU.subtract)
                    v.drain()
                    v.tensor_copy(piece[2], sq[0:Q])
                    v.drain()

            def chunk(k, s, pair):
                m = steps3(msg[s])
                v.wait_ge(aux_rdy[k], pair * 2 + (s + 1))
                v.wait_ge(gathered[k][s], (pair + 1) * (16 * STEPS))
                if k in (L1A, L1B):
                    v.tensor_tensor(m, m, w_c[s][:, :].unsqueeze(2).to_broadcast([P, STEPS, D]), ALU.mult)
                    v.drain()
                if k == L2:
                    f = frow3(s)
                    v.wait_ge(frow_in[s], (pair + 1) * 16)
                    for t in range(STEPS):
                        v.scalar_tensor_tensor(f[:, t, :], dstate[:, :] if t == 0 else f[:, t - 1, :],
                                               same_c[s][:, t:t + 1], f[:, t, :], ALU.mult, ALU.add)
                        v.scalar_tensor_tensor(m[:, t, :], rows[:, ROW_E, :], w_c[s][:, t:t + 1], m[:, t, :],
                                               ALU.mult, ALU.add)
                        v.drain()
                    v.tensor_tensor(m, m, f, ALU.add)
                    v.tensor_copy(dstate[:, :], f[:, STEPS - 1, :])
                    v.drain()
                    v.tensor_scalar(m, m, 0.0, None, ALU.max)
                    v.drain()
                for t in range(STEPS):
                    v.scalar_tensor_tensor(m[:, t, :], state[:, :] if t == 0 else m[:, t - 1, :],
                                           same_c[s][:, t:t + 1], m[:, t, :], ALU.mult, ALU.add)
                    v.drain()
                v.tensor_copy(state[:, :], m[:, STEPS - 1, :])
                v.drain()
                v.sem_inc(summed[k], 1)

            def to_cat(k, g):
                tot = total[g % 2][0:Q]
                if k in WITH_CAT and k != L1B:
                    if (k, g) != (L0, 0):
                        v.wait_ge(turned, count(WITH_CAT, k, g) - 1)
                    if k == L0:
                        v.tensor_tensor(cat[0:Q, :, D:2 * D], tot, per_node(dinv, g), ALU.mult)
                        v.tensor_copy(cat[0:Q, :, 0:D], grp(xcur, g))
                    elif k == L2:
                        v.tensor_tensor(cat[0:Q, :, 0:D], tot, per_node(has, g), ALU.mult)
                    else:
                        v.tensor_tensor(cat[0:Q, :, 0:D], tot, per_node(dinv, g), ALU.mult)
                        v.tensor_copy(cat[0:Q, :, D:2 * D], grp(xcur, g))
                    v.drain()
                    v.sem_inc(cat_rdy, 1)

            def join(k, g, mode):
                m = GATHER[mode].index(k)
                v.wait_ge(ends_in[g], 16 * GT * (m + 1))
                v.wait_ge(spilled, m * GROUPS + g + 1)
                v.tensor_tensor(total[g % 2][0:Q], grp(ends, g), ps3(ps_spill[(m * GROUPS + g) % 2], D), ALU.add)
                v.drain()
                v.sem_inc(joined, 1)
                to_cat(k, g)

            def take_sums(k, g):
                for b in range(GT):
                    p = ps_sum[SUM_BANK[b]]
                    v.wait_ge(dense_done, before(LINEAR["linear"], k) * NPP + g * GT + b + 1)
                    if MATRIX[k] == COUNTS:
                        v.tensor_reduce(total[g % 2][0:Q, b, :],
                                        p[0:Q, 0:3 * D].rearrange("p (c d) -> p d c", d=D), AX.X, ALU.add)\
                         .then_inc(dense_used, 1)
                    else:
                        v.tensor_copy(total[g % 2][0:Q, b, :], p[0:Q, 0:D]).then_inc(dense_used, 1)
                v.drain()
                to_cat(k, g)

            def layernorm(k, g):
                rq, sqq, st = r[0:Q], sq[0:Q], stat[0:Q]
                bc = stat[0:Q, :].unsqueeze(2).to_broadcast([Q, GT, D])
                v.tensor_reduce(st, rq, AX.X, ALU.add)
                v.drain()
                v.tensor_scalar(st, st, -1.0 / D, None, ALU.mult)
                v.drain()
                v.tensor_tensor(rq, rq, bc, ALU.add)
                v.drain()
                v.tensor_tensor(sqq, rq, rq, ALU.mult)
                v.drain()
                v.tensor_reduce(var[0:Q], sqq, AX.X, ALU.add).then_inc(var_rdy, 1)
                v.wait_ge(std_rdy, count(WITH_LN, k, g))
                v.reciprocal(st, std[0:Q])
                v.drain()
                v.tensor_tensor(grp(xcur, g), rq, bc, ALU.mult)
                v.drain()

            def finish(k, g, mode):
                tot, rq, sqq = total[g % 2][0:Q], r[0:Q], sq[0:Q]
                if k == L0:
                    v.wait_ge(prod, count(WITH_CAT, k, g))
                    v.tensor_tensor(rq, ps3(ps_o, D), grp(keep, g), ALU.add)
                    v.drain()
                    v.sem_inc(prod_used, 1)
                    layernorm(k, g)
                    v.tensor_tensor(grp(tab1, g), grp(xcur, g), per_node(norm, g), ALU.mult)
                    v.drain()
                    v.sem_inc(tab_rdy, 1)
                elif k == L1A:
                    v.tensor_tensor(tot, tot, per_node(norm_has, g), ALU.mult)
                    v.drain()
                    if g == 0 and k - 1 in TO_DRAM[mode]:
                        v.wait_ge(tab_out, 16 * GROUPS)
                    v.tensor_tensor(grp(tab_out_of(k, mode), g), tot, per_node(norm, g), ALU.mult)
                    v.tensor_tensor(grp(keep, g), tot, grp(xcur, g), ALU.add)
                    v.drain()
                    v.sem_inc(tab_rdy, 1)
                elif k == L1B:
                    v.tensor_tensor(rq, tot, per_node(norm_has, g), ALU.mult)
                    v.drain()
                    v.tensor_tensor(rq, rq, grp(keep, g), ALU.add)
                    v.drain()
                    v.scalar_tensor_tensor(rq, rq, 1.0 / 3.0, grp(xcur, g), ALU.mult, ALU.add)
                    v.drain()
                    layernorm(k, g)
                    v.wait_ge(turned, count(WITH_CAT, k, g) - 1)
                    v.tensor_copy(cat[0:Q, :, 0:D], grp(xcur, g))
                    v.drain()
                    v.sem_inc(cat_rdy, 1)
                elif k == L2:
                    v.tensor_tensor(sqq, row_bc(ROW_B2), per_node(deg, g), ALU.mult)
                    v.drain()
                    v.tensor_tensor(sqq, sqq, grp(xcur, g), ALU.add)
                    v.drain()
                    v.wait_ge(prod, count(WITH_CAT, k, g))
                    v.tensor_tensor(rq, ps3(ps_o, D), sqq, ALU.add)
                    v.drain()
                    v.sem_inc(prod_used, 1)
                    layernorm(k, g)
                    if mode == "linear":
                        split(xcur, g * GT, (g + 1) * GT)
                    v.sem_inc(tab_rdy, 1)
                elif k == L3A:
                    v.wait_ge(prod_tab, count(TAB_ACT, k, g))
                    v.tensor_tensor(rq, ps3(ps_o, 2 * D)[:, :, D:2 * D], row_bc(ROW_B3), ALU.add)
                    v.drain()
                    v.sem_inc(prod_used, 1)
                    v.tensor_tensor(grp(keep, g), rq, grp(xcur, g), ALU.add)
                    v.drain()
                elif k == L3B:
                    v.tensor_tensor(rq, tot, per_node(dinv, g), ALU.mult)
                    v.drain()
                    v.tensor_tensor(rq, rq, grp(keep, g), ALU.add)
                    v.drain()
                    layernorm(k, g)
                    v.sem_inc(tab_rdy, 1)

            def dst_half(g):
                v.wait_ge(prod_tab, count(TAB_ACT, L1B, g))
                v.tensor_tensor(half_of(g), ps3(ps_o, 2 * D)[:, :, D:2 * D], row_bc(ROW_B1), ALU.add)
                v.drain()
                v.sem_inc(prod_used, 1)

            def half_of(g):
                return grp(keep, g)

            def run(mode):
                if mode == "linear":
                    keys()
                    one_hot()
                if mode == "linear":
                    v.wait_ge(grp_done, 2 * BATCH + NGROUPS)
                    v.wait_ge(pool_rdy, 2 * TURNS * ITB)
                v.tensor_tensor(keep[0:Q], xcur[0:Q], row_bc(ROW_B0, NPP), ALU.add)
                v.drain()
                if mode == "linear":
                    split(xcur, 0, NPP)
                    v.sem_inc(parts_rdy, 1)
                for k in range(PASSES):
                    if k in GATHER[mode]:
                        m = GATHER[mode].index(k)
                        if m:
                            v.wait_ge(spilled, m * GROUPS)
                        if k == L2 and mode == "linear":
                            fill_spill(2)
                        v.memset(state[:, :], 0.0)
                        v.memset(dstate[:, :], 0.0)
                        v.drain()
                        with v.Fori(0, PAIRS) as pair:
                            for s in range(2):
                                chunk(k, s, pair)
                        join(k, 0, mode)
                    for g in range(GROUPS):
                        if k in GATHER[mode]:
                            if g + 1 < GROUPS:
                                join(k, g + 1, mode)
                        else:
                            take_sums(k, g)
                        finish(k, g, mode)
                        if k == L1B:
                            dst_half(g)
                    if k == L1B:
                        v.tensor_copy(drow[0:Q], keep[0:Q])
                        v.drain()
                        v.sem_inc(drow_rdy, GROUPS)
                    if k == L2 and mode == "linear":
                        v.sem_inc(parts_rdy, 1)
                    if k == L3A and mode == "linear":
                        v.wait_ge(prod_tab, 2 * GROUPS)
                        split(tab1, 0, NPP)
                        v.sem_inc(parts_rdy, 1)

            both(v, run)


MAX_GROUP = SLOTS


_INS = ["x", "src", "dst", "edge_weight", "edge_weight1", "L0_gnn_W", "L0_gnn_b", "L2_gnn_W1", "L2_gnn_b1",
        "L2_gnn_W2", "L2_gnn_b2", "L3_gnn_W1_l", "L3_gnn_b1", "L3_gnn_W1_r", "L3_gnn_W2_l", "L3_gnn_b2",
        "L3_gnn_W2_r"]


def kernel(**inputs):
    import numpy as _np
    import concourse.bacc as _bacc
    from concourse.bass_utils import run_bass_kernel_spmd as _run

    nc = _bacc.Bacc("TRN2", target_bir_lowering=False, num_devices=1)
    arrays, args = {}, []
    for name in _INS:
        a = _np.ascontiguousarray(inputs[name])
        if name == "edge_weight1":
            a = a.reshape(-1)
        arrays[f"in_{name}"] = a
        args.append(nc.dram_tensor(f"in_{name}", a.shape, mybir.dt.from_np(a.dtype), kind="ExternalInput").ap())
    out = nc.dram_tensor("out_x", arrays["in_x"].shape, F32, kind="ExternalOutput").ap()
    build_program(nc, *args, out)
    return _run(nc, [arrays], core_ids=[0]).results[0]["out_x"]
```

```python
from contextlib import ExitStack

import concourse.bass as bass
from concourse import mybir

F32 = mybir.dt.float32
BF16 = mybir.dt.bfloat16
F16 = mybir.dt.float16
I32 = mybir.dt.int32
ALU = mybir.AluOpType
ACT = mybir.ActivationFunctionType
AX = mybir.AxisListType

P = 128
Q = 125
D = 64
HID = 128
STEPS = 34
GNODES = 5
SLOTS = 256
EPS = 1e-5
PASSES = 6
L0, L1A, L1B, L2, L3A, L3B = range(PASSES)


def build_program(nc, x, src, dst, edge_w, edge_e, L0_W, L0_b, L2_W1, L2_b1, L2_W2, L2_b2,
                  L3_W1_l, L3_b1, L3_W1_r, L3_W2_l, L3_b2, L3_W2_r, out):
    N_NODES = x.shape[0]
    N_EDGES = src.shape[0]
    EPP = -(-N_EDGES // (P * 2 * STEPS)) * 2 * STEPS
    EDGES = P * EPP
    TAIL = N_EDGES - (P - 1) * EPP
    CHUNKS = EPP // STEPS
    PAIRS = CHUNKS // 2
    NPP = N_NODES // Q
    GT = 5
    GROUPS = NPP // GT
    BPP = 4
    BLK = EPP // BPP
    BLOCKS = P * BPP
    NO_NODE = 8191.0
    PART_ONE = 10
    RING = 11
    ZROWS = 23
    ZSTORES = EPP // ZROWS
    HALVES = SLOTS // P
    NGROUPS = N_NODES // GNODES
    GBLK = NGROUPS // Q
    COLS = NPP * GNODES
    BATCH = 5
    BT = BATCH * HALVES
    GPB = Q // GNODES
    ITG = 2 * GPB
    ITB = ITG // BATCH
    TURNS = NGROUPS // ITG
    DVE_COLS = 80
    BANK = 512
    BUILD_BANKS = 5
    FAR = 10000.0
    AROW = NPP * Q
    assert 0 < TAIL <= EPP and NPP * Q == N_NODES and GT * GROUPS == NPP and BPP * BLK == EPP
    assert ZSTORES * ZROWS == EPP and RING * BLK <= 2 * STEPS * D and GT * D <= BANK and N_NODES < NO_NODE
    assert NGROUPS * GNODES == N_NODES and GBLK * Q == NGROUPS and TURNS * ITG == NGROUPS
    assert GROUPS % 2 == 0 and COLS <= 256 and ITG % BUILD_BANKS == 0 and ITB % 2 == 0 and ZSTORES == 2 * (TURNS + GROUPS - 1)

    COUNTS, WEIGHTS = "counts", "weights"
    MATRIX = {L0: COUNTS, L1A: WEIGHTS, L1B: WEIGHTS, L3A: COUNTS, L3B: COUNTS}

    def dram(name, shape, dt=F32):
        return nc.dram_tensor(name, shape, dt, kind="Internal").ap()

    running = dram("running", (EDGES, D))
    running_w = dram("running_w", (EDGES, 1))
    first_rows = dram("first_rows", (EDGES + N_NODES, D))
    dst_blocks = dram("dst_blocks", (BLOCKS, BLK))
    edges_upto = dram("edges_upto", (N_NODES + 2 * GNODES,))
    packed = [dram(f"packed{i}", (EDGES + SLOTS, 1)) for i in range(3)]
    tables = [x] + [dram(f"table{k}", (N_NODES, D)) for k in range(1, PASSES)]
    dst_table = dram("dst_table", (N_NODES, D))
    a_dram = {COUNTS: dram("a_counts", (NPP, P, AROW), BF16), WEIGHTS: dram("a_weights", (NPP, P, AROW))}

    def tiles_of(table, g):
        return table.rearrange("(j q) d -> q j d", q=Q)[:, g * GT:(g + 1) * GT, :]

    with ExitStack() as ctx:
        def sb(name, shape, dt=F32):
            return ctx.enter_context(nc.sbuf_tensor(name, shape, dt))

        def sem(name):
            return ctx.enter_context(nc.semaphore(name))

        stream = sb("stream", [P, 3 * AROW])
        node_room = sb("node_room", [P, 3 * NPP * D])
        SETF = BT * P * 4 // 2 + BT * COLS // 2
        operand_room = sb("operand_room", [P, 2 * SETF])

        def in_room(room, at, n, dt=F32):
            words = n if dt in (F32, I32) else n // 2
            piece = room[:, at:at + words]
            return piece if dt == F32 else piece.bitcast(dt)

        stage = {WEIGHTS: [in_room(stream, b * AROW, AROW) for b in range(2)],
                 COUNTS: [in_room(stream, 2 * AROW + b * AROW // 2, AROW, BF16) for b in range(2)]}
        a_buf = {WEIGHTS: [in_room(stream, b * AROW, AROW) for b in range(3)],
                 COUNTS: [in_room(stream, b * AROW // 2, AROW, BF16) for b in range(GT)]}
        A_SLOT = {WEIGHTS: [0, 1, 2, 0, 1], COUNTS: [0, 1, 2, 3, 4]}
        CH = STEPS * D
        msg = [in_room(stream, s * CH, CH) for s in range(2)]
        frow = in_room(stream, 2 * CH, 2 * CH)
        spill = in_room(stream, 4 * CH, NPP * Q).rearrange("p (j q) -> p j q", q=Q)
        dst_all = in_room(stream, 0, EPP)
        dst_int = in_room(stream, CH, EPP, I32)
        ends = in_room(node_room, 0, NPP * D).rearrange("p (j d) -> p j d", d=D)
        tab1 = in_room(node_room, NPP * D, NPP * D).rearrange("p (j d) -> p j d", d=D)
        keep = in_room(node_room, 2 * NPP * D, NPP * D).rearrange("p (j d) -> p j d", d=D)
        tab0 = ends
        NT = NGROUPS * HALVES
        key_t = in_room(node_room, 0, NT)
        lo_t = in_room(node_room, NT, NT, BF16)
        wp_t = [in_room(node_room, NT + (i + 1) * NT // 2, NT, BF16) for i in range(3)]
        e_tmp = [in_room(node_room, i * EPP, EPP) for i in range(6)]
        onehot = [[in_room(operand_room, b * SETF + i * BT * P // 2, BT * P, BF16)
                   .rearrange("p (c t) -> p c t", t=BT) for i in range(4)] for b in range(2)]
        high = [in_room(operand_room, b * SETF + 2 * BT * P, BT * COLS, BF16)
                .rearrange("p (t c) -> p t c", c=COLS) for b in range(2)]
        group_rows = [in_room(operand_room, i * SLOTS, SLOTS) for i in range(6)]
        PART = NPP // 2
        DVE_SPLITS = (1, 3, 5, 7)
        NORM_AT = 4
        SHARE = NPP - 10
        PWORDS = PART * 3 * D // 2
        parts = {k: [in_room(room, at, PART * 3 * D, BF16).rearrange("p (j c) -> p j c", c=3 * D)
                     for room, at in places]
                 for k, places in ((L0, ((operand_room, 0), (operand_room, PWORDS))),
                                   (L3A, ((operand_room, 0), (operand_room, PWORDS))),
                                   (L3B, ((operand_room, 2 * PWORDS), (node_room, 0))))}
        rest_l3 = in_room(node_room, PWORDS, GT * D).rearrange("p (j d) -> p j d", d=D)

        src_all = sb("src_all", [P, EPP], I32)
        same_all = sb("same_all", [P, EPP])
        w_all = sb("w_all", [P, EPP])
        idx_c = [sb(f"idx_c{s}", [P, STEPS], I32) for s in range(2)]
        same_c = [sb(f"same_c{s}", [P, STEPS]) for s in range(2)]
        w_c = [sb(f"w_c{s}", [P, STEPS]) for s in range(2)]
        state = sb("state", [P, D])
        dstate = sb("dstate", [P, D])
        xcur = sb("xcur", [P, NPP, D])
        total = [sb(f"total{i}", [P, GT, D]) for i in range(2)]
        node_i = sb("node_i", [P, NPP], I32)
        blk_i = sb("blk_i", [P, NPP], I32)
        end_i = sb("end_i", [P, NPP], I32)
        start_i = sb("start_i", [P, NPP], I32)
        node_f, blk_f, cnt, upto, below, deg, has, dinv, norm, norm_has, tmpn, wend, wcarry = (
            sb(n, [P, NPP]) for n in ("node_f", "blk_f", "cnt", "upto", "below", "deg", "has", "dinv", "norm",
                                      "norm_has", "tmpn", "wend", "wcarry"))
        gstart, gend, gcnt, gbase = (sb(n, [P, GBLK]) for n in ("gstart", "gend", "gcnt", "gbase"))
        gstart_i = sb("gstart_i", [P, GBLK], I32)
        gbase_i = sb("gbase_i", [P, GBLK], I32)
        first_i = sb("first_i", [P, 1], I32)
        next_f, cont, last_f, last_w, eps1, gmax = (
            sb(n, [P, 1]) for n in ("next_f", "cont", "last_f", "last_w", "eps1", "gmax"))
        flag_f = sb("flag_f", [1, 1])
        flag_i = sb("flag_i", [1, 1], I32)
        zeros = sb("zeros", [P, ZROWS * D])
        b0row = sb("b0row", [P, D])
        junk = sb("junk", [P, BLOCKS])
        firsts = in_room(operand_room, 0, BLOCKS)
        firsts_d = in_room(operand_room, BLOCKS, BLOCKS).rearrange("p (b q) -> p b q", q=P)
        ident = sb("ident", [P, P])
        ones = sb("ones", [P, P])
        low_iota = sb("low_iota", [P, P * BT], BF16).rearrange("p (c t) -> p c t", t=BT)
        high_iota = sb("high_iota", [P, 256], F16)
        slot_f = sb("slot_f", [P, SLOTS])
        slot_i = in_room(operand_room, 2 * BLOCKS, SLOTS, I32)
        cat = sb("cat", [P, GT, 2 * D])
        catT = sb("catT", [P, GT, P])
        hidT = sb("hidT", [P, GT, P])
        sumT = hidT
        r = sb("r", [P, GT, D])
        sq = sb("sq", [P, GT, D])
        stat = sb("stat", [P, GT])
        var = sb("var", [P, GT])
        std = sb("std", [P, GT])
        w0 = sb("w0", [D, 2 * D])
        w0T = sb("w0T", [2 * D, D])
        wab = sb("wab", [D, 2 * D])
        w2 = sb("w2", [D, D])
        w3 = sb("w3", [2 * D, HID])
        w3lr = sb("w3lr", [HID, 2 * D])
        b3 = sb("b3", [HID, 1])
        rows = sb("rows", [P, 5, D])
        ROW_B0, ROW_B1, ROW_B2, ROW_B3, ROW_E = range(5)

        ps = ctx.enter_context(nc.psum_tensor("ps", [P, 8 * BANK], F32))

        def bank(b, n=1):
            return ps[:, b * BANK:(b + n) * BANK]

        ps_sum = [bank(b) for b in range(3)]
        ps_spill = [bank(3), bank(2)]
        ps_t = bank(4, 2)
        ps_o = bank(6, 2)
        ps_pack = [bank(b) for b in (5, 6, 7)]
        SUM_BANK = [0, 1, 2, 0, 1]

        filled = sem("filled")
        consts = sem("consts")
        dst_in = sem("dst_in")
        src_in = sem("src_in")
        w_in = sem("w_in")
        e_in = sem("e_in")
        x_in = sem("x_in")
        wts_in = sem("wts_in")
        dst_float = sem("dst_float")
        same_rdy = sem("same_rdy")
        dblk_out = sem("dblk_out")
        next_in = sem("next_in")
        firsts_rdy = sem("firsts_rdy")
        firsts_ps = sem("firsts_ps")
        blk_rdy = sem("blk_rdy")
        blk_row = [sem(f"blk_row{i}") for i in range(RING)]
        blk_used = sem("blk_used")
        pack_rdy = sem("pack_rdy")
        pack_out = sem("pack_out")
        upto_rdy = sem("upto_rdy")
        upto_out = sem("upto_out")
        below_in = sem("below_in")
        end_rdy = sem("end_rdy")
        wend_in = sem("wend_in")
        spill_rdy = sem("spill_rdy")
        wspill = sem("wspill")
        wdeg_rdy = sem("wdeg_rdy")
        norm_root = sem("norm_root")
        gmax_rdy = sem("gmax_rdy")
        gmax_ps = sem("gmax_ps")
        flag_rdy = sem("flag_rdy")
        start_done = sem("start_done")
        w0_ps = sem("w0_ps")
        w0_rdy = sem("w0_rdy")
        zero_out = sem("zero_out")
        group_in = sem("group_in")
        group_rdy = sem("group_rdy")
        group_ps = sem("group_ps")
        group_used = sem("group_used")
        lo_rdy = sem("lo_rdy")
        ops_rdy = sem("ops_rdy")
        pool_rdy = sem("pool_rdy")
        grp_done = sem("grp_done")
        evac = sem("evac")
        stage_out = [sem(f"stage_out{b}") for b in range(2)]
        stage_free = sem("stage_free")
        a_in = [sem(f"a_in{b}") for b in range(GT)]
        dense_done = sem("dense_done")
        dense_used = sem("dense_used")
        sums_sb = sem("sums_sb")
        sums_turned = sem("sums_turned")
        sums_taken = sem("sums_taken")
        parts_rdy = sem("parts_rdy")
        aux_rdy = [sem(f"aux_rdy{k}") for k in range(PASSES)]
        pool_go = sem("pool_go")
        pe_go = sem("pe_go")
        gathered = [[sem(f"gathered{k}_{s}") for s in range(2)] for k in range(PASSES)]
        summed = [sem(f"summed{k}") for k in range(PASSES)]
        stored = [[sem(f"stored{k}_{s}") for s in range(2)] for k in range(PASSES)]
        msg_used = sem("msg_used")
        frow_in = [sem(f"frow_in{s}") for s in range(2)]
        spill_num = sem("spill_num")
        ends_in = [sem(f"ends_in{g}") for g in range(GROUPS)]
        spilled = sem("spilled")
        joined = sem("joined")
        cat_rdy = sem("cat_rdy")
        turned = sem("turned")
        turned_sb = sem("turned_sb")
        hid_ps = sem("hid_ps")
        hid_sb = sem("hid_sb")
        prod = sem("prod")
        prod_used = sem("prod_used")
        prod_tab = sem("prod_tab")
        var_rdy = sem("var_rdy")
        std_rdy = sem("std_rdy")
        tab_rdy = sem("tab_rdy")
        tab_out = sem("tab_out")
        drow_rdy = sem("drow_rdy")
        drow_out = sem("drow_out")
        scattered = sem("scattered")
        b0_in = sem("b0_in")
        b0_out = sem("b0_out")
        out_done = sem("out_done")

        block = ctx.enter_context(nc.Block())

        WITH_CAT = (L0, L1B, L2, L3A)
        WITH_HID = (L3A,)
        WITH_LN = (L0, L1B, L2, L3B)
        TAB_DVE = (L0, L1A, L2, L3B)
        TAB_ACT = (L1B, L3A)
        GATHER = {"linear": (L2,), "gather": (L0, L1A, L1B, L2, L3A, L3B)}
        LINEAR = {m: tuple(k for k in range(PASSES) if k not in GATHER[m]) for m in GATHER}
        TO_DRAM = {m: tuple(k - 1 for k in GATHER[m] if k > 0) for m in GATHER}

        def count(users, k, g):
            return users.index(k) * GROUPS + g + 1

        def before(users, k):
            return sum(u < k for u in users)

        def steps3(tile):
            return tile.rearrange("p (t d) -> p t d", d=D)

        def frow3(s):
            return steps3(frow[:, s * CH:(s + 1) * CH])

        def ps3(p, w, n=GT):
            return p[0:Q, 0:n * w].rearrange("p (j d) -> p j d", d=w)

        def per_node(col, g, w=D):
            return col[0:Q, g * GT:(g + 1) * GT].unsqueeze(2).to_broadcast([Q, GT, w])

        def row_bc(i, n=GT):
            return rows[0:Q, i:i + 1, :].to_broadcast([Q, n, D])

        def grp(tile, g):
            return tile[0:Q, g * GT:(g + 1) * GT, :]

        def tab_out_of(k, mode):
            return tab0 if k == L1A and mode == "linear" else tab1

        def tab_in_of(k):
            return {L1A: tab1, L1B: tab0}[k]

        def split(eng, k, table, rest, lo, hi):
            half = parts[k][lo // PART]
            piece = [half[0:Q, lo % PART:lo % PART + hi - lo, i * D:(i + 1) * D] for i in range(3)]
            eng.tensor_copy(piece[0], table)
            eng.drain()
            eng.tensor_tensor(rest, table, piece[0], ALU.subtract)
            eng.drain()
            eng.tensor_copy(piece[1], rest)
            eng.drain()
            eng.tensor_tensor(rest, rest, piece[1], ALU.subtract)
            eng.drain()
            eng.tensor_copy(piece[2], rest)
            eng.drain()
            eng.sem_inc(parts_rdy, 1)

        def both(eng, run):
            eng.wait_ge(flag_rdy, 1)
            fits = eng.value_load(flag_i[0:1, 0:1], min_val=0, max_val=1)
            with eng.If(fits):
                run("linear")
            with eng.Else():
                run("gather")
            eng.drain()

        @block.sync
        def _(sp):
            def load_edges(tile, flat, signal):
                main = flat[0:(P - 1) * EPP].rearrange("(p t) -> p t", p=P - 1)
                sp.dma_start(tile[0:P - 1, :], main).then_inc(signal, 16)
                last = flat[(P - 1) * EPP:N_EDGES].rearrange("(p t) -> p t", p=1)
                sp.dma_start(tile[P - 1:P, 0:TAIL], last).then_inc(signal, 16)

            sp.wait_ge(filled, 1)
            load_edges(dst_int, dst, dst_in)
            sp.wait_ge(filled, 3)
            load_edges(w_all, edge_w, w_in)
            load_edges(src_all, src, src_in)
            sp.dma_start(xcur[0:Q, :, :], x.rearrange("(j q) d -> q j d", q=Q)).then_inc(x_in, 16)
            sp.wait_ge(dst_float, 1)
            sp.dma_start(dst_blocks.rearrange("(p b) t -> p (b t)", p=P), dst_all[:, :]).then_inc(dblk_out, 16)
            sp.wait_ge(filled, 5)
            sp.dma_start(next_f[0:P - 1, :], dst_all[1:P, 0:1]).then_inc(next_in, 16)
            sp.wait_ge(pack_rdy, 1)
            for i, tile in enumerate((e_tmp[0], e_tmp[1], w_all)):
                sp.dma_start(packed[i][0:EDGES, :].rearrange("(p t) a -> p (t a)", p=P), tile[:, :])\
                  .then_inc(pack_out, 16)
                sp.dma_start(packed[i][EDGES:EDGES + SLOTS, :].rearrange("(p t) a -> p (t a)", p=1),
                             zeros[0:1, 0:SLOTS]).then_inc(pack_out, 16)
            sp.dma_start(running_w.rearrange("(p t) a -> p (t a)", p=P), e_tmp[2][:, :]).then_inc(pack_out, 16)
            sp.wait_ge(upto_rdy, 1)
            sp.dma_start(edges_upto[1:N_NODES + 1].rearrange("(j q) -> q j", q=Q), upto[0:Q, :],
                         allow_slow_non_contiguous=True).then_inc(upto_out, 16)
            sp.dma_start(edges_upto[0:1].rearrange("(p j) -> p j", p=1), zeros[0:1, 0:1]).then_inc(upto_out, 16)
            sp.wait_ge(upto_out, 32)
            sp.dma_start(below[0:Q, :], edges_upto[0:N_NODES].rearrange("(j q) -> q j", q=Q),
                         allow_slow_non_contiguous=True).then_inc(below_in, 16)
            for tile, at in ((gstart, 0), (gend, GNODES)):
                groups = edges_upto[at:at + N_NODES].rearrange("(b q r) -> q b r", q=Q, r=GNODES)
                sp.dma_start(tile[0:Q, :], groups[:, :, 0], allow_slow_non_contiguous=True).then_inc(below_in, 16)

            flat_first = first_rows[0:EDGES, :].rearrange("(p t) d -> p (t d)", p=P)

            def zero_first(n):
                sp.dma_start(flat_first[:, bass.ds(n * (ZROWS * D), ZROWS * D)], zeros[:, :]).then_inc(zero_out, 16)

            def store_matrices():
                with sp.Fori(0, TURNS) as i:
                    for b in range(2):
                        sp.wait_ge(evac, i * ITG + (BUILD_BANKS + (b + 1) * GPB))
                        for what in (WEIGHTS, COUNTS):
                            to = a_dram[what].rearrange("j p c -> p j c")[:, bass.ds(i * 2 + b, 1), :]
                            sp.dma_start(to, stage[what][b][:, :].unsqueeze(1)).then_inc(stage_out[b], 16)
                        zero_first(i * 2 + b)
                    for b in range(2):
                        sp.wait_ge(stage_out[b], (i + 1) * 32)
                        sp.sem_inc(stage_free, 1)

            def load_a(k, g):
                what = MATRIX[k]
                base = before(LINEAR["linear"], k) * NPP
                first = isinstance(g, int) and g == 0
                for b in range(GT):
                    if what == WEIGHTS and b >= 3:
                        sp.wait_ge(dense_done, g * GT + (base + b - 2))
                    elif k == L1A and first:
                        sp.wait_ge(dense_done, base - GT + (2, 4, 5)[b])
                    elif k == L3A and first:
                        if b == 0:
                            for s in range(2):
                                sp.wait_ge(stored[L2][s], 16 * PAIRS)
                        if b == 2:
                            sp.wait_ge(spilled, GROUPS)
                    elif not (k == L0 and first):
                        last = {WEIGHTS: (3, 4, 2, 3, 4), COUNTS: range(GT)}[what][b]
                        sp.wait_ge(dense_done, g * GT + (base + last + 1 - GT))
                    sp.dma_start(a_buf[what][A_SLOT[what][b]][:, :].unsqueeze(1),
                                 a_dram[what].rearrange("j p c -> p j c")[:, bass.ds(g * GT + b, 1), :])\
                      .then_inc(a_in[b], 16)

            def store(k, s, pair):
                rows_of = running.rearrange("(p t) d -> p (t d)", p=P)
                sp.wait_ge(summed[k], 2 * pair + s + 1)
                source = frow[:, s * CH:(s + 1) * CH] if k == L2 else msg[s][:, :]
                sp.dma_start(rows_of[:, bass.ds((2 * pair + s) * CH, CH)], source).then_inc(stored[k][s], 16)

            def load_first(s, pair):
                sp.dma_start(frow[:, s * CH:(s + 1) * CH],
                             flat_first[:, bass.ds((2 * pair + s) * CH, CH)]).then_inc(frow_in[s], 16)

            def store_nodes(k, g, mode):
                if k in TO_DRAM[mode]:
                    if k in TAB_DVE:
                        sp.wait_ge(tab_rdy, count(TAB_DVE, k, g))
                    else:
                        sp.wait_ge(prod_tab, count(TAB_ACT, k, g))
                    source = xcur if k == L2 else tab_out_of(k, mode)
                    sp.dma_start(tiles_of(tables[k + 1], g), grp(source, g)).then_inc(tab_out, 16)
                if k == L1B:
                    sp.wait_ge(drow_rdy, g + 1)
                    sp.dma_start(tiles_of(dst_table, g), grp(keep, g)).then_inc(drow_out, 16)
                if k == L3B:
                    sp.wait_ge(tab_rdy, count(TAB_DVE, k, g))
                    sp.dma_start(tiles_of(out, g), grp(xcur, g)).then_inc(out_done, 16)

            def run(mode):
                if mode == "linear":
                    store_matrices()
                else:
                    with sp.Fori(0, ZSTORES) as n:
                        zero_first(n)
                for k in range(PASSES):
                    if k in GATHER[mode]:
                        if k == L2:
                            load_edges(w_all, edge_e, e_in)
                            sp.wait_ge(scattered, 16 * NPP)
                            sp.wait_ge(b0_in, 16)
                            sp.dma_start(steps3(flat_first)[:, 0, :], b0row[:, :]).then_inc(b0_out, 16)
                            sp.wait_ge(b0_out, 16)
                            load_first(0, 0)
                            load_first(1, 0)
                        with sp.Fori(0, PAIRS - 1) as pair:
                            for s in range(2):
                                store(k, s, pair)
                                if k == L2:
                                    sp.wait_ge(stored[k][s], pair * 16 + 16)
                                    load_first(s, pair + 1)
                        for s in range(2):
                            store(k, s, PAIRS - 1)
                        for g in range(GROUPS):
                            store_nodes(k, g, mode)
                    else:
                        load_a(k, 0)
                        if k in (L1B, L3B):
                            for g in range(1, GROUPS):
                                load_a(k, g)
                                store_nodes(k, g - 1, mode)
                            store_nodes(k, GROUPS - 1, mode)
                        else:
                            with sp.Fori(1, GROUPS) as g:
                                load_a(k, g)
                                if k == L1A:
                                    for n in range(2):
                                        zero_first(g * 2 + (2 * TURNS - 2 + n))
                sp.wait_ge(out_done, 16 * GROUPS)
                sp.wait_ge(zero_out, 16 * ZSTORES)

            both(sp, run)

        @block.gpsimd
        def _(pool):
            def numbers(tile, pattern):
                return pool.iota(tile, pattern=pattern, base=0, channel_multiplier=0)

            pool.memset(dst_int[:, :], int(NO_NODE)).then_inc(filled, 1)
            pool.memset(src_all[:, :], 0).then_inc(filled, 1)
            pool.memset(w_all[:, :], 0.0).then_inc(filled, 1)
            pool.memset(zeros[:, :], 0.0).then_inc(filled, 1)
            pool.memset(next_f[:, :], -1.0).then_inc(filled, 1)
            pool.memset(ident[:, :], 0.0).then_inc(consts, 1)
            pool.memset(ones[:, :], 1.0).then_inc(consts, 1)
            pool.memset(eps1[:, :], EPS).then_inc(consts, 1)
            pool.iota(node_i[:, :], pattern=[[Q, NPP]], base=0, channel_multiplier=1).then_inc(consts, 1)
            pool.iota(gbase_i[:, :], pattern=[[GNODES * Q, GBLK]], base=0, channel_multiplier=GNODES)\
                .then_inc(consts, 1)
            numbers(slot_i[:, :], [[1, SLOTS]]).then_inc(consts, 1)
            pool.wait_ge(consts, 6)
            pool.affine_select(out=ident[:, :], in_=ident[:, :], compare_op=ALU.not_equal, fill=1.0, base=0,
                               pattern=[[-1, P]], channel_multiplier=1).then_inc(consts, 1)
            numbers(spill.bitcast(I32), [[Q, NPP], [1, Q]]).then_inc(spill_num, 1)

            pool.wait_ge(dblk_out, 16)
            for j in range(NPP):
                if j % PART_ONE == 0:
                    pool.wait_ge(blk_rdy, j // PART_ONE + 1)
                if j >= RING:
                    pool.wait_ge(blk_used, j - RING + 1)
                pool.indirect_dma_start(frow[0:Q, (j % RING) * BLK:(j % RING + 1) * BLK], None, dst_blocks[:, :],
                                        bass.IndirectOffsetOnAxis(blk_i[0:Q, j:j + 1], 0))\
                    .then_inc(blk_row[j % RING], 16)

            def gather_weights():
                pool.wait_ge(pack_out, 16 * 7)
                pool.wait_ge(end_rdy, 1)
                for j in range(NPP):
                    pool.indirect_dma_start(wend[0:Q, j:j + 1], None, running_w[:, :],
                                            bass.IndirectOffsetOnAxis(end_i[0:Q, j:j + 1], 0)).then_inc(wend_in, 16)

            def gather_groups():
                for b in range(GBLK):
                    if b >= 2:
                        pool.wait_ge(group_ps, b - 1)
                    for i in range(3):
                        pool.indirect_dma_start(group_rows[(b % 2) * 3 + i][0:Q, :], None, packed[i][:, :],
                                                bass.IndirectOffsetOnAxis(gstart_i[0:Q, b:b + 1], 0))\
                            .then_inc(group_in, 16)
                    pool.wait_ge(group_in, 48 * (b + 1))

            def build_part():
                with pool.Fori(0, TURNS) as i:
                    for bt in range(ITB):
                        pool.wait_ge(lo_rdy, i * ITB + (bt + 1))
                        pool.sem_inc(pool_go, 1)
                        at = bass.ds(i * (ITB * BT) + bt * BT, BT)
                        for part, lo in ((1, DVE_COLS), (2, 0)):
                            ins = pool.tensor_tensor(
                                onehot[bt % 2][1 + part][:, lo:Q, :], onehot[bt % 2][0][:, lo:Q, :],
                                wp_t[part][:, at].unsqueeze(1).to_broadcast([P, Q - lo, BT]), ALU.mult)
                        ins.then_inc(pool_rdy, 1)

            def gather_chunk(k, s):
                for t in range(STEPS):
                    pool.indirect_dma_start(steps3(msg[s])[:, t, :], None, tables[k][:, :],
                                            bass.IndirectOffsetOnAxis(idx_c[s][:, t:t + 1], 0))\
                        .then_inc(gathered[k][s], 16)

            def run(mode):
                if mode == "linear":
                    gather_groups()
                    build_part()
                    pool.wait_ge(ops_rdy, TURNS * ITB)
                    pool.wait_ge(grp_done, 2 * BATCH + NGROUPS)
                    split(pool, L0, xcur[0:Q, SHARE:NPP, :], tab1[0:Q, SHARE:NPP, :], SHARE, NPP)
                gather_weights()
                for k in GATHER[mode]:
                    if k == L2:
                        pool.wait_ge(zero_out, 16 * ZSTORES)
                        for j in range(NPP):
                            if j % GT == 0:
                                pool.wait_ge(drow_rdy, j // GT + 1)
                            pool.indirect_dma_start(first_rows[:, :],
                                                    bass.IndirectOffsetOnAxis(start_i[0:Q, j:j + 1], 0),
                                                    keep[0:Q, j, :], None).then_inc(scattered, 16)
                        pool.wait_ge(drow_out, 16 * GROUPS)
                        pool.indirect_dma_start(b0row[:, :], None, dst_table[:, :],
                                                bass.IndirectOffsetOnAxis(first_i[:, 0:1], 0)).then_inc(b0_in, 16)
                    if k > 0:
                        pool.wait_ge(tab_out, 16 * GROUPS * (TO_DRAM[mode].index(k - 1) + 1))
                    for s in range(2):
                        pool.wait_ge(aux_rdy[k], s + 1)
                        gather_chunk(k, s)
                    if mode == "linear":
                        numbers(spill.bitcast(I32), [[Q, NPP], [1, Q]]).then_inc(spill_num, 1)
                    with pool.Fori(0, PAIRS - 1) as pair:
                        for s in range(2):
                            if k == L2:
                                pool.wait_ge(msg_used, pair * 2 + (s + 1))
                            else:
                                pool.wait_ge(stored[k][s], (pair + 1) * 16)
                            pool.wait_ge(aux_rdy[k], pair * 2 + (s + 3))
                            pool.sem_inc(pool_go, 1)
                            gather_chunk(k, s)
                    for s in range(2):
                        pool.wait_ge(stored[k][s], 16 * PAIRS)
                    if GATHER[mode].index(k):
                        pool.wait_ge(joined, GATHER[mode].index(k) * GROUPS)
                    for j in range(NPP):
                        pool.indirect_dma_start(ends[0:Q, j, :], None, running[:, :],
                                                bass.IndirectOffsetOnAxis(end_i[0:Q, j:j + 1], 0))\
                            .then_inc(ends_in[j // GT], 16)
                if mode == "linear":
                    for g in range(GROUPS):
                        if g in DVE_SPLITS:
                            continue
                        pool.wait_ge(tab_rdy, count(TAB_DVE, L2, g))
                        split(pool, L3A, grp(xcur, g), grp(tab1, g), g * GT, (g + 1) * GT)
                    for g in range(GROUPS):
                        pool.wait_ge(prod_tab, count(TAB_ACT, L3A, g))
                        split(pool, L3B, grp(tab1, g), rest_l3[0:Q], g * GT, (g + 1) * GT)

            both(pool, run)

        @block.scalar
        def _(act):
            act.dma_start(w0[:, :], L0_W).then_inc(wts_in, 16)
            act.dma_start(wab[:, 0:D], L2_W1[0:D, :]).then_inc(wts_in, 16)
            act.dma_start(wab[:, D:2 * D], L2_W1[D:2 * D, :]).then_inc(wts_in, 16)
            act.dma_start(w2[:, :], L2_W2).then_inc(wts_in, 16)
            act.dma_start(w3[0:D, :], L3_W1_l).then_inc(wts_in, 16)
            act.dma_start(w3[D:2 * D, :], L3_W1_r).then_inc(wts_in, 16)
            act.dma_start(w3lr[:, 0:D], L3_W2_l).then_inc(wts_in, 16)
            act.dma_start(w3lr[:, D:2 * D], L3_W2_r).then_inc(wts_in, 16)
            act.dma_start(b3[:, :], L3_b1.rearrange("(p a) -> p a", a=1)).then_inc(wts_in, 16)
            for i, b in ((ROW_B0, L0_b), (ROW_B1, L2_b1), (ROW_B2, L2_b2), (ROW_B3, L3_b2)):
                act.dma_start(rows[:, i, :], b.partition_broadcast(P)).then_inc(wts_in, 16)
            act.dma_start(rows[:, ROW_E, :], L2_W1[2 * D, :].partition_broadcast(P)).then_inc(wts_in, 16)
            act.wait_ge(w0_ps, 1)
            act.copy(w0T[:, :], ps_t[:, 0:D]).then_inc(w0_rdy, 1)

            def copy_out():
                act.sem_inc(evac, BUILD_BANKS)
                act.sem_inc(stage_free, 2)
                with act.Fori(0, TURNS) as i:
                    for gi in range(ITG):
                        b, at = gi // GPB, (gi % GPB) * GNODES
                        if gi % GPB == 0:
                            act.wait_ge(stage_free, i * 2 + (b + 1))
                        act.wait_ge(grp_done, i * ITG + (2 * BATCH + gi + 1))
                        for what, col in ((COUNTS, 0), (WEIGHTS, 256)):
                            place = stage[what][b].rearrange("p (h q) -> p h q", q=Q)[:, :, at:at + GNODES]
                            psum = bank(gi % BUILD_BANKS)[:, col:col + COLS].rearrange("p (h r) -> p h r", r=GNODES)
                            ins = act.copy(place, psum)
                        ins.then_inc(evac, 1)

            def aux(k, s, pair):
                at = bass.ds((2 * pair + s) * STEPS, STEPS)
                if k in (L1A, L1B, L2):
                    act.copy(w_c[s][:, :], w_all[:, at])
                act.copy(same_c[s][:, :], same_all[:, at])
                act.copy(idx_c[s][:, :], src_all[:, at])
                act.drain()
                act.sem_inc(aux_rdy[k], 1)

            def root(k, g):
                act.wait_ge(var_rdy, count(WITH_LN, k, g))
                act.activation(std[0:Q, :], var[0:Q, :], ACT.Sqrt, bias=eps1[0:Q, :], scale=1.0 / D)\
                   .then_inc(std_rdy, 1)

            def nodes(k, g, mode):
                if k in LINEAR[mode] and MATRIX[k] == WEIGHTS:
                    m = (L1A, L1B).index(k) * GROUPS + g
                    if m:
                        act.wait_ge(sums_turned, m)
                    for b in range(GT):
                        act.wait_ge(dense_done, before(LINEAR[mode], k) * NPP + g * GT + b + 1)
                        act.copy(sumT[0:D, b, 0:Q], ps_sum[SUM_BANK[b]][0:D, 0:Q]).then_inc(dense_used, 1)
                    act.drain()
                    act.sem_inc(sums_sb, 1)
                if k == L1B:
                    root(k, g)
                if k in WITH_CAT:
                    kr = D if k in (L1B, L2) else 2 * D
                    act.wait_ge(turned, count(WITH_CAT, k, g))
                    if (k, g) != (WITH_CAT[0], 0):
                        act.wait_ge(prod, count(WITH_CAT, k, g) - 1)
                    act.copy(catT[0:kr, :, 0:Q], ps_t[0:kr, 0:GT * P].rearrange("p (j c) -> p j c", c=P)[:, :, 0:Q])\
                       .then_inc(turned_sb, 1)
                if k in WITH_HID:
                    act.wait_ge(hid_ps, count(WITH_HID, k, g))
                    act.activation(hidT[:, :, 0:Q], ps_t[:, 0:GT * P].rearrange("p (j c) -> p j c", c=P)[:, :, 0:Q],
                                   ACT.Relu, bias=b3[:, :]).then_inc(hid_sb, 1)
                if k in TAB_ACT:
                    act.wait_ge(prod, count(WITH_CAT, k, g))
                    act.copy(grp(tab1, g), ps3(ps_o, 2 * D)[:, :, 0:D]).then_inc(prod_tab, 1)
                if k in (L0, L2, L3B):
                    root(k, g)
                if k == L0 and g == NORM_AT:
                    act.wait_ge(wdeg_rdy, 1)
                    act.activation(norm[0:Q, :], tmpn[0:Q, :], ACT.Sqrt).then_inc(norm_root, 1)

            def run(mode):
                if mode == "linear":
                    copy_out()
                for k in range(PASSES):
                    if k in GATHER[mode]:
                        if GATHER[mode].index(k):
                            act.wait_ge(summed[k - 1], CHUNKS)
                        if k == L2:
                            act.wait_ge(e_in, 32)
                        aux(k, 0, 0)
                        aux(k, 1, 0)
                        with act.Fori(0, PAIRS - 1) as pair:
                            for s in range(2):
                                act.wait_ge(summed[k], pair * 2 + (s + 1))
                                aux(k, s, pair + 1)
                    for g in range(GROUPS):
                        nodes(k, g, mode)

            act.wait_ge(src_in, 32)
            both(act, run)

        @block.tensor
        def _(pe):
            pe.wait_ge(firsts_rdy, 1)
            pe.matmul(ps_o[:, 0:BLOCKS], ones[:, :], firsts_d[:, :, :].rearrange("p b q -> p (b q)"),
                      start=True, stop=True).then_inc(firsts_ps, 1)
            pe.wait_ge(wts_in, 14 * 16)
            pe.transpose(ps_t[:, 0:D], w0[:, :], ident[0:D, 0:D]).then_inc(w0_ps, 1)
            pe.wait_ge(spill_rdy, 1)
            for j in range(NPP):
                ins = pe.matmul(bank(3)[0:Q, j:j + 1], spill[:, j, :], last_w[:, :], start=True, stop=True)
            ins.then_inc(wspill, 1)
            pe.wait_ge(gmax_rdy, 1)
            pe.transpose(bank(2)[0:1, 0:Q], gmax[0:Q, :], ident[0:Q, 0:Q]).then_inc(gmax_ps, 1)
            pe.wait_ge(w0_rdy, 1)

            def turn_groups():
                for b in range(GBLK):
                    pe.wait_ge(group_rdy, b + 1)
                    if b:
                        pe.wait_ge(group_used, b)
                    for i in range(3):
                        for h in range(HALVES):
                            ins = pe.transpose(ps_pack[i][:, h * Q:(h + 1) * Q],
                                               group_rows[(b % 2) * 3 + i][0:Q, h * P:(h + 1) * P], ident[0:Q, 0:Q])
                    ins.then_inc(group_ps, 1)

            def build():
                pe.sem_inc(grp_done, 2 * BATCH)
                with pe.Fori(0, TURNS) as i:
                    for gi in range(ITG):
                        bt, s = gi // BATCH, (gi // BATCH) % 2
                        if gi % BATCH == 0:
                            pe.wait_ge(ops_rdy, i * ITB + (bt + 1))
                            pe.wait_ge(pool_rdy, i * ITB + (bt + 1))
                        pe.wait_ge(evac, i * ITG + (gi + 1))
                        out_bank = bank(gi % BUILD_BANKS)
                        tiles = [(gi % BATCH) * HALVES + h for h in range(HALVES)]
                        for t in tiles:
                            pe.matmul(out_bank[:, 0:COLS], onehot[s][0][:, :, t], high[s][:, t, :],
                                      start=t == tiles[0], stop=t == tiles[-1])
                        for t in tiles:
                            for part in range(3):
                                ins = pe.matmul(out_bank[:, 256:256 + COLS], onehot[s][1 + part][:, :, t],
                                                high[s][:, t, :], start=(t, part) == (tiles[0], 0),
                                                stop=(t, part) == (tiles[-1], 2))
                        ins.then_inc(grp_done, 1)

            def dense(k, g, between=()):
                what = MATRIX[k]
                lin = before(LINEAR["linear"], k)
                for b in range(GT):
                    pe.wait_ge(a_in[b], g * 16 + (lin * GROUPS + 1) * 16)
                    used = lin * NPP + b + (-2 if b >= 3 else (3, 4, 2)[b] - b - GT + 1)
                    if isinstance(g, int) and g == 0 and used <= 0:
                        pass
                    else:
                        pe.wait_ge(dense_used, g * GT + used)
                    a = a_buf[what][A_SLOT[what][b]].rearrange("p (h q) -> p h q", q=Q)
                    for h in range(NPP):
                        if what == COUNTS:
                            ins = pe.matmul(ps_sum[SUM_BANK[b]][0:Q, 0:3 * D], a[0:Q, h, :],
                                            parts[k][h // PART][0:Q, h % PART, :],
                                            start=h == 0, stop=h == NPP - 1)
                        else:
                            ins = pe.matmul(ps_sum[SUM_BANK[b]][0:D, 0:Q], tab_in_of(k)[0:Q, h, :], a[0:Q, h, :],
                                            start=h == 0, stop=h == NPP - 1)
                    ins.then_inc(dense_done, 1)
                    if b < len(between):
                        between[b]()

            def turn(k, g, back=0):
                m = (L1A, L1B).index(k) * GROUPS - back
                pe.wait_ge(sums_sb, g + (m + 1))
                if not (isinstance(g, int) and g + m == 0):
                    pe.wait_ge(sums_taken, g + m)
                pe.sem_inc(pe_go, 1)
                for b in range(GT):
                    ins = pe.transpose(bank(3)[0:Q, b * D:(b + 1) * D], sumT[0:D, b, 0:Q], ident[0:D, 0:D])
                ins.then_inc(sums_turned, 1)

            def carry(k, g, mode):
                n = GATHER[mode].index(k) * GROUPS + g
                pe.wait_ge(summed[k], CHUNKS)
                if k == L2 and mode == "linear":
                    pe.wait_ge(spill_rdy, 2)
                if n >= 2:
                    pe.wait_ge(joined, n - 1)
                for j in range(GT):
                    ins = pe.matmul(ps_spill[n % 2][0:Q, j * D:(j + 1) * D], spill[:, g * GT + j, :], state[:, :],
                                    start=True, stop=True)
                ins.then_inc(spilled, 1)

            def node_steps(k, g, mode, back=0):
                done = g + ((WITH_CAT.index(k) * GROUPS if k in WITH_CAT else 0) - back)
                first = isinstance(g, int) and done == 0
                kr = D if k in (L1B, L2) else 2 * D

                def turn_rows():
                    pe.wait_ge(cat_rdy, done + 1)
                    if not first:
                        pe.wait_ge(turned_sb, done)
                    pe.sem_inc(pe_go, 1)
                    for j in range(GT):
                        ins = pe.transpose(ps_t[0:kr, j * P:j * P + Q], cat[0:Q, j, 0:kr], ident[0:Q, 0:Q])
                    ins.then_inc(turned, 1)

                def hidden():
                    pe.wait_ge(turned_sb, done + 1)
                    ps_tt = ps_t[:, 0:GT * P].rearrange("p (j c) -> p j c", c=P)
                    for lo, hi in ((0, 4), (4, GT)):
                        ins = pe.matmul(ps_tt[:, lo:hi, 0:Q], w3[:, :], catT[:, lo:hi, 0:Q], start=True, stop=True)
                    ins.then_inc(hid_ps, 1)

                def product():
                    if k in WITH_HID:
                        pe.wait_ge(hid_sb, g + (1 - back))
                    else:
                        pe.wait_ge(turned_sb, done + 1)
                    if not first:
                        pe.wait_ge(prod_used, done)
                    for j in range(GT):
                        if k == L0:
                            ins = pe.matmul(ps_o[0:Q, j * D:(j + 1) * D], catT[:, j, 0:Q], w0T[:, :],
                                            start=True, stop=True)
                        elif k == L1B:
                            ins = pe.matmul(ps_o[0:Q, j * P:(j + 1) * P], catT[0:D, j, 0:Q], wab[:, :],
                                            start=True, stop=True)
                        elif k == L2:
                            ins = pe.matmul(ps_o[0:Q, j * D:(j + 1) * D], catT[0:D, j, 0:Q], w2[:, :],
                                            start=True, stop=True)
                        else:
                            ins = pe.matmul(ps_o[0:Q, j * P:(j + 1) * P], hidT[:, j, 0:Q], w3lr[:, :],
                                            start=True, stop=True)
                    ins.then_inc(prod, 1)

                steps = [lambda: turn(k, g, back)] if k in (L1A, L1B) and mode == "linear" else []
                if k in WITH_CAT:
                    steps += [turn_rows, hidden, product] if k in WITH_HID else [turn_rows, product]
                return steps

            def run(mode):
                if mode == "linear":
                    turn_groups()
                    build()
                for k in range(PASSES):
                    if k in GATHER[mode]:
                        carry(k, 0, mode)
                        carry(k, 1, mode)
                        for g in range(GROUPS):
                            for step in node_steps(k, g, mode):
                                step()
                            if g + 2 < GROUPS:
                                carry(k, g + 2, mode)
                    else:
                        if MATRIX[k] == COUNTS:
                            pe.wait_ge(parts_rdy, {L0: 3, L3A: 3 + GROUPS, L3B: 3 + 2 * GROUPS}[k])
                        else:
                            pe.wait_ge(tab_rdy, (TAB_DVE.index(k - 1) + 1) * GROUPS)
                        dense(k, 0)
                        peeled = 2 if k in (L0, L1A) else 1
                        for g in range(1, peeled):
                            dense(k, g, node_steps(k, g, mode, back=1))
                        with pe.Fori(peeled, GROUPS) as g:
                            dense(k, g, node_steps(k, g, mode, back=1))
                        for step in node_steps(k, GROUPS - 1, mode):
                            step()

            both(pe, run)

        @block.vector
        def _(v):
            v.wait_ge(dst_in, 32)
            v.tensor_copy(dst_all[:, :], dst_int[:, :]).then_inc(dst_float, 1)
            v.memset(same_all[:, 0:1], 0.0)
            v.drain()
            v.tensor_tensor(same_all[:, 1:EPP], dst_all[:, 1:EPP], dst_all[:, 0:EPP - 1], ALU.is_equal)
            v.wait_ge(consts, 7)
            for b in range(BPP):
                v.tensor_scalar(firsts_d[:, b, :], ident[:, :], dst_all[:, b * BLK:b * BLK + 1], None, ALU.mult)
            v.tensor_copy(node_f[:, :], node_i[:, :])
            v.tensor_copy(first_i[:, :], dst_all[:, 0:1])
            v.tensor_copy(last_f[:, :], dst_all[:, EPP - 1:EPP])
            v.tensor_copy(slot_f[:, :], slot_i[:, :])
            v.tensor_copy(low_iota, slot_i[:, 0:P].unsqueeze(2).to_broadcast([P, P, BT]))
            v.tensor_copy(high_iota[:, :], slot_i[:, 0:256])
            v.tensor_copy(gbase[:, :], gbase_i[:, :])
            v.drain()
            v.sem_inc(firsts_rdy, 1)
            v.wait_ge(firsts_ps, 1)
            v.tensor_copy(firsts[:, :], ps_o[:, 0:BLOCKS])
            v.drain()
            for a in range(0, NPP, PART_ONE):
                for j in range(a, a + PART_ONE):
                    v.tensor_scalar(junk[:, 0:BLOCKS], firsts[:, :], node_f[:, j:j + 1], None, ALU.is_le, ALU.add,
                                    accum_out=cnt[:, j:j + 1])
                    v.drain()
                some = slice(a, a + PART_ONE)
                v.tensor_scalar(blk_f[:, some], cnt[:, some], -1.0, 0.0, ALU.add, ALU.max)
                v.drain()
                v.tensor_copy(blk_i[:, some], blk_f[:, some]).then_inc(blk_rdy, 1)
            hd, lo, run_w, hi, off, fsrc = e_tmp
            hi_int = off.bitcast(I32)

            def divide():
                v.wait_ge(src_in, 32)
                v.tensor_copy(fsrc, src_all[:, :])
                v.drain()
                v.tensor_scalar(hi, fsrc, 1.0 / Q, None, ALU.mult)
                v.drain()
                v.tensor_copy(hi_int, hi)
                v.drain()
                v.tensor_copy(hi, hi_int)
                v.drain()
                v.scalar_tensor_tensor(lo, hi, -float(Q), fsrc, ALU.mult, ALU.add)
                v.drain()

            def correct():
                v.tensor_scalar(off, lo, 0.0, None, ALU.is_lt)
                v.tensor_scalar(hd, lo, float(Q), None, ALU.is_ge)
                v.drain()
                v.tensor_tensor(off, hd, off, ALU.subtract)
                v.drain()
                v.tensor_tensor(hi, hi, off, ALU.add)
                v.scalar_tensor_tensor(lo, off, -float(Q), lo, ALU.mult, ALU.add)
                v.drain()
                v.scalar_tensor_tensor(hd, hi, float(GNODES), dst_all[:, :], ALU.mult, ALU.add)

            def running_weights():
                v.wait_ge(w_in, 32)
                v.tensor_tensor_scan(run_w, same_all[:, :], w_all[:, :], 0.0, ALU.mult, ALU.add)
                v.drain()
                v.tensor_copy(last_w[:, :], run_w[:, EPP - 1:EPP])
                v.drain()
                v.wait_ge(filled, 4)
                v.sem_inc(pack_rdy, 1)

            def fill_spill(n):
                v.wait_ge(spill_num, n)
                v.tensor_scalar(spill, spill.bitcast(I32), last_f[:, :], cont[:, 0:1], ALU.is_equal, ALU.mult)\
                 .then_inc(spill_rdy, 1)

            v.wait_ge(next_in, 16)
            v.tensor_tensor(cont[:, :], next_f[:, :], last_f[:, :], ALU.is_equal)
            v.drain()
            for j in range(NPP):
                v.wait_ge(blk_row[j % RING], 16 * (j // RING + 1))
                v.tensor_scalar(junk[0:Q, 0:BLK], frow[0:Q, (j % RING) * BLK:(j % RING + 1) * BLK],
                                node_f[0:Q, j:j + 1], None, ALU.is_le, ALU.add, accum_out=cnt[0:Q, j:j + 1])\
                 .then_inc(blk_used, 1)
                v.drain()
                if j == 2:
                    divide()
                if j == 12:
                    correct()
                if j == 22:
                    running_weights()
                if j == 32:
                    fill_spill(1)

            def n(tile):
                return tile[0:Q, :]

            v.scalar_tensor_tensor(n(upto), n(blk_f), float(BLK), n(cnt), ALU.mult, ALU.add).then_inc(upto_rdy, 1)
            v.drain()
            v.tensor_scalar(n(tmpn), n(upto), -1.0, 0.0, ALU.add, ALU.max)
            v.drain()
            v.tensor_copy(n(end_i), n(tmpn)).then_inc(end_rdy, 1)
            v.wait_ge(below_in, 48)
            v.tensor_tensor(n(deg), n(upto), n(below), ALU.subtract)
            v.tensor_tensor(n(gcnt), n(gend), n(gstart), ALU.subtract)
            v.tensor_copy(n(gstart_i), n(gstart))
            v.drain()
            v.tensor_reduce(n(gmax), n(gcnt), AX.X, ALU.max).then_inc(gmax_rdy, 1)
            v.tensor_scalar(n(has), n(deg), 1.0, None, ALU.min)
            v.tensor_scalar(n(dinv), n(deg), 1.0, None, ALU.max)
            v.tensor_scalar(n(cnt), n(node_f), float(EDGES), None, ALU.add)
            v.drain()
            v.reciprocal(n(dinv), n(dinv))
            v.tensor_tensor(n(below), n(below), n(cnt), ALU.subtract)
            v.drain()
            v.tensor_tensor(n(dinv), n(dinv), n(has), ALU.mult)
            v.tensor_tensor(n(below), n(below), n(has), ALU.mult)
            v.drain()
            v.tensor_tensor(n(below), n(below), n(cnt), ALU.add)
            v.drain()
            v.tensor_copy(n(start_i), n(below))
            v.wait_ge(gmax_ps, 1)
            v.tensor_reduce(flag_f[:, :], bank(2)[0:1, 0:Q], AX.X, ALU.max)
            v.drain()
            v.tensor_scalar(flag_f[:, :], flag_f[:, :], float(MAX_GROUP), None, ALU.is_le)
            v.drain()
            v.tensor_copy(flag_i[:, :], flag_f[:, :])
            v.wait_ge(wspill, 1)
            v.tensor_copy(n(wcarry), bank(3)[0:Q, 0:NPP])
            v.wait_ge(pack_out, 16 * 7)
            v.wait_ge(x_in, 16)
            v.wait_ge(wts_in, 14 * 16)
            v.drain()
            v.sem_inc(flag_rdy, 1)

            def norms():
                v.wait_ge(wend_in, 16 * NPP)
                v.tensor_tensor(n(wend), n(wend), n(wcarry), ALU.add)
                v.drain()
                v.tensor_tensor(n(wend), n(wend), n(has), ALU.mult)
                v.drain()
                v.tensor_scalar(n(tmpn), n(wend), 1.0, None, ALU.max).then_inc(wdeg_rdy, 1)
                v.wait_ge(norm_root, 1)
                v.reciprocal(n(norm), n(norm))
                v.drain()
                v.tensor_tensor(n(norm_has), n(norm), n(has), ALU.mult)
                v.drain()

            def keys():
                def t3(tile, b):
                    piece = tile.rearrange("p (g h) -> p g h", h=HALVES)[:, b * Q:(b + 1) * Q, :]
                    return piece.rearrange("p g h -> p h g")

                for b in range(GBLK):
                    key = group_rows[(b % 2) * 3]
                    v.wait_ge(group_in, 48 * (b + 1))
                    v.tensor_scalar(junk[0:Q, 0:SLOTS], slot_f[0:Q, :], gcnt[0:Q, b:b + 1], FAR, ALU.is_ge, ALU.mult)
                    v.drain()
                    v.scalar_tensor_tensor(key[0:Q, :], key[0:Q, :], gbase[0:Q, b:b + 1], junk[0:Q, 0:SLOTS],
                                           ALU.subtract, ALU.add)
                    v.drain()
                    v.sem_inc(group_rdy, 1)
                    v.wait_ge(group_ps, b + 1)
                    p3 = [p[:, 0:HALVES * Q].rearrange("p (h g) -> p h g", g=Q) for p in ps_pack]
                    rest = junk[:, 0:HALVES * Q].rearrange("p (h g) -> p h g", g=Q)
                    v.tensor_copy(t3(key_t, b), p3[0])
                    v.tensor_copy(t3(lo_t, b), p3[1])
                    v.tensor_copy(t3(wp_t[0], b), p3[2])
                    v.drain()
                    v.tensor_tensor(rest, p3[2], t3(wp_t[0], b), ALU.subtract)
                    v.drain()
                    v.sem_inc(group_used, 1)
                    v.tensor_copy(t3(wp_t[1], b), rest)
                    v.drain()
                    v.tensor_tensor(rest, rest, t3(wp_t[1], b), ALU.subtract)
                    v.drain()
                    v.tensor_copy(t3(wp_t[2], b), rest)
                    v.drain()

            def one_hot():
                v.wait_ge(group_ps, GBLK)
                for tile in onehot[0] + onehot[1]:
                    v.memset(tile[:, Q:P, :], 0.0)
                v.drain()
                with v.Fori(0, TURNS) as i:
                    for bt in range(ITB):
                        s, at = bt % 2, bass.ds(i * (ITB * BT) + bt * BT, BT)
                        for gi in range(BATCH):
                            v.wait_ge(grp_done, i * ITG + (bt * BATCH + gi + 1))
                            for t in range(gi * HALVES, (gi + 1) * HALVES):
                                col = bass.ds(i * (ITB * BT) + (bt * BT + t), 1)
                                v.tensor_scalar(high[s][:, t, :], high_iota[:, 0:COLS], key_t[:, col], None,
                                                ALU.is_equal)
                        v.tensor_tensor(onehot[s][0][:, 0:Q, :], low_iota[:, 0:Q, :],
                                        lo_t[:, at].unsqueeze(1).to_broadcast([P, Q, BT]),
                                        ALU.is_equal).then_inc(lo_rdy, 1)
                        v.drain()
                        for part in range(2):
                            cols = (Q, DVE_COLS)[part]
                            v.tensor_tensor(onehot[s][1 + part][:, 0:cols, :], onehot[s][0][:, 0:cols, :],
                                            wp_t[part][:, at].unsqueeze(1).to_broadcast([P, cols, BT]), ALU.mult)
                        v.drain()
                        v.sem_inc(ops_rdy, 1)

            def chunk(k, s, pair):
                m = steps3(msg[s])
                v.wait_ge(aux_rdy[k], pair * 2 + (s + 1))
                if k == L2:
                    f = frow3(s)
                    v.wait_ge(frow_in[s], (pair + 1) * 16)
                    for t in range(STEPS):
                        v.scalar_tensor_tensor(f[:, t, :], dstate[:, :] if t == 0 else f[:, t - 1, :],
                                               same_c[s][:, t:t + 1], f[:, t, :], ALU.mult, ALU.add)
                        v.drain()
                    v.tensor_copy(dstate[:, :], f[:, STEPS - 1, :])
                    v.drain()
                    for t in range(STEPS):
                        v.scalar_tensor_tensor(f[:, t, :], rows[:, ROW_E, :], w_c[s][:, t:t + 1], f[:, t, :],
                                               ALU.mult, ALU.add)
                    v.drain()
                v.wait_ge(gathered[k][s], (pair + 1) * (16 * STEPS))
                if k in (L1A, L1B):
                    v.tensor_tensor(m, m, w_c[s][:, :].unsqueeze(2).to_broadcast([P, STEPS, D]), ALU.mult)
                    v.drain()
                if k == L2:
                    v.tensor_tensor(f, m, f, ALU.add).then_inc(msg_used, 1)
                    v.drain()
                    m = f
                    v.tensor_scalar(m, m, 0.0, None, ALU.max)
                    v.drain()
                for t in range(STEPS):
                    v.scalar_tensor_tensor(m[:, t, :], state[:, :] if t == 0 else m[:, t - 1, :],
                                           same_c[s][:, t:t + 1], m[:, t, :], ALU.mult, ALU.add)
                    v.drain()
                v.tensor_copy(state[:, :], m[:, STEPS - 1, :])
                v.drain()
                v.sem_inc(summed[k], 1)

            def to_cat(k, g):
                tot = total[g % 2][0:Q]
                if k in WITH_CAT and k != L1B:
                    if (k, g) != (L0, 0):
                        v.wait_ge(turned, count(WITH_CAT, k, g) - 1)
                    if k == L0:
                        v.tensor_tensor(cat[0:Q, :, D:2 * D], tot, per_node(dinv, g), ALU.mult)
                        v.tensor_copy(cat[0:Q, :, 0:D], grp(xcur, g))
                    elif k == L2:
                        v.tensor_tensor(cat[0:Q, :, 0:D], tot, per_node(has, g), ALU.mult)
                    else:
                        v.tensor_tensor(cat[0:Q, :, 0:D], tot, per_node(dinv, g), ALU.mult)
                        v.tensor_copy(cat[0:Q, :, D:2 * D], grp(xcur, g))
                    v.drain()
                    v.sem_inc(cat_rdy, 1)

            def join(k, g, mode):
                m = GATHER[mode].index(k)
                v.wait_ge(ends_in[g], 16 * GT * (m + 1))
                v.wait_ge(spilled, m * GROUPS + g + 1)
                v.tensor_tensor(total[g % 2][0:Q], grp(ends, g), ps3(ps_spill[(m * GROUPS + g) % 2], D), ALU.add)
                v.drain()
                v.sem_inc(joined, 1)
                to_cat(k, g)

            def take_sums(k, g):
                if MATRIX[k] == WEIGHTS:
                    v.wait_ge(sums_turned, (L1A, L1B).index(k) * GROUPS + g + 1)
                    v.tensor_copy(total[g % 2][0:Q], ps3(bank(3), D)).then_inc(sums_taken, 1)
                for b in range(GT if MATRIX[k] == COUNTS else 0):
                    v.wait_ge(dense_done, before(LINEAR["linear"], k) * NPP + g * GT + b + 1)
                    v.tensor_reduce(total[g % 2][0:Q, b, :],
                                    ps_sum[SUM_BANK[b]][0:Q, 0:3 * D].rearrange("p (c d) -> p d c", d=D),
                                    AX.X, ALU.add).then_inc(dense_used, 1)
                v.drain()
                to_cat(k, g)

            def layernorm(k, g):
                rq, sqq, st = r[0:Q], sq[0:Q], stat[0:Q]
                bc = stat[0:Q, :].unsqueeze(2).to_broadcast([Q, GT, D])
                v.tensor_reduce(st, rq, AX.X, ALU.add)
                v.drain()
                v.tensor_scalar(st, st, -1.0 / D, None, ALU.mult)
                v.drain()
                v.tensor_tensor(rq, rq, bc, ALU.add)
                v.drain()
                v.tensor_tensor(sqq, rq, rq, ALU.mult)
                v.drain()
                v.tensor_reduce(var[0:Q], sqq, AX.X, ALU.add).then_inc(var_rdy, 1)
                v.wait_ge(std_rdy, count(WITH_LN, k, g))
                v.reciprocal(st, std[0:Q])
                v.drain()
                v.tensor_tensor(grp(xcur, g), rq, bc, ALU.mult)
                v.drain()

            def finish(k, g, mode):
                tot, rq, sqq = total[g % 2][0:Q], r[0:Q], sq[0:Q]
                if k == L0:
                    v.wait_ge(prod, count(WITH_CAT, k, g))
                    v.tensor_tensor(rq, ps3(ps_o, D), grp(keep, g), ALU.add)
                    v.drain()
                    v.sem_inc(prod_used, 1)
                    layernorm(k, g)
                    if g == NORM_AT:
                        norms()
                    if g >= NORM_AT:
                        for done in range(g + 1) if g == NORM_AT else (g,):
                            v.tensor_tensor(grp(tab1, done), grp(xcur, done), per_node(norm, done), ALU.mult)
                        v.drain()
                        v.sem_inc(tab_rdy, g + 1 if g == NORM_AT else 1)
                elif k == L1A:
                    v.tensor_tensor(tot, tot, per_node(norm_has, g), ALU.mult)
                    v.drain()
                    if g == 0 and k - 1 in TO_DRAM[mode]:
                        v.wait_ge(tab_out, 16 * GROUPS)
                    v.tensor_tensor(grp(tab_out_of(k, mode), g), tot, per_node(norm, g), ALU.mult)
                    v.tensor_tensor(grp(keep, g), tot, grp(xcur, g), ALU.add)
                    v.drain()
                    v.sem_inc(tab_rdy, 1)
                elif k == L1B:
                    v.tensor_tensor(rq, tot, per_node(norm_has, g), ALU.mult)
                    v.drain()
                    v.tensor_tensor(rq, rq, grp(keep, g), ALU.add)
                    v.drain()
                    v.scalar_tensor_tensor(rq, rq, 1.0 / 3.0, grp(xcur, g), ALU.mult, ALU.add)
                    v.drain()
                    layernorm(k, g)
                    v.wait_ge(turned, count(WITH_CAT, k, g) - 1)
                    v.tensor_copy(cat[0:Q, :, 0:D], grp(xcur, g))
                    v.drain()
                    v.sem_inc(cat_rdy, 1)
                elif k == L2:
                    v.tensor_tensor(sqq, row_bc(ROW_B2), per_node(deg, g), ALU.mult)
                    v.drain()
                    v.tensor_tensor(sqq, sqq, grp(xcur, g), ALU.add)
                    v.drain()
                    v.wait_ge(prod, count(WITH_CAT, k, g))
                    v.tensor_tensor(rq, ps3(ps_o, D), sqq, ALU.add)
                    v.drain()
                    v.sem_inc(prod_used, 1)
                    layernorm(k, g)
                    if mode == "linear" and g in DVE_SPLITS:
                        split(v, L3A, grp(xcur, g), sqq, g * GT, (g + 1) * GT)
                    v.sem_inc(tab_rdy, 1)
                elif k == L3A:
                    v.wait_ge(prod_tab, count(TAB_ACT, k, g))
                    v.tensor_tensor(rq, ps3(ps_o, 2 * D)[:, :, D:2 * D], row_bc(ROW_B3), ALU.add)
                    v.drain()
                    v.sem_inc(prod_used, 1)
                    v.tensor_tensor(grp(keep, g), rq, grp(xcur, g), ALU.add)
                    v.drain()
                elif k == L3B:
                    v.tensor_tensor(rq, tot, per_node(dinv, g), ALU.mult)
                    v.drain()
                    v.tensor_tensor(rq, rq, grp(keep, g), ALU.add)
                    v.drain()
                    layernorm(k, g)
                    v.sem_inc(tab_rdy, 1)

            def dst_half(g):
                v.wait_ge(prod_tab, count(TAB_ACT, L1B, g))
                v.tensor_tensor(grp(keep, g), ps3(ps_o, 2 * D)[:, :, D:2 * D], row_bc(ROW_B1), ALU.add)
                v.drain()
                v.sem_inc(prod_used, 1)
                v.sem_inc(drow_rdy, 1)

            def run(mode):
                if mode == "linear":
                    keys()
                    one_hot()
                if mode == "linear":
                    v.wait_ge(grp_done, 2 * BATCH + NGROUPS)
                    v.wait_ge(pool_rdy, TURNS * ITB)
                    for lo, hi in ((0, PART), (PART, SHARE)):
                        split(v, L0, xcur[0:Q, lo:hi, :], tab1[0:Q, lo:hi, :], lo, hi)
                v.tensor_tensor(keep[0:Q], xcur[0:Q], row_bc(ROW_B0, NPP), ALU.add)
                v.drain()
                for k in range(PASSES):
                    if k in GATHER[mode]:
                        m = GATHER[mode].index(k)
                        if m:
                            v.wait_ge(spilled, m * GROUPS)
                        v.memset(state[:, :], 0.0)
                        v.memset(dstate[:, :], 0.0)
                        v.drain()
                        for s in range(2):
                            chunk(k, s, 0)
                        if mode == "linear":
                            fill_spill(2)
                        with v.Fori(1, PAIRS) as pair:
                            for s in range(2):
                                chunk(k, s, pair)
                        join(k, 0, mode)
                    for g in range(GROUPS):
                        if k in GATHER[mode]:
                            if g + 1 < GROUPS:
                                join(k, g + 1, mode)
                        else:
                            take_sums(k, g)
                        finish(k, g, mode)
                        if k == L1B:
                            dst_half(g)

            both(v, run)


MAX_GROUP = SLOTS


_INS = ["x", "src", "dst", "edge_weight", "edge_weight1", "L0_gnn_W", "L0_gnn_b", "L2_gnn_W1", "L2_gnn_b1",
        "L2_gnn_W2", "L2_gnn_b2", "L3_gnn_W1_l", "L3_gnn_b1", "L3_gnn_W1_r", "L3_gnn_W2_l", "L3_gnn_b2",
        "L3_gnn_W2_r"]


def kernel(**inputs):
    import numpy as _np
    import concourse.bacc as _bacc
    from concourse.bass_utils import run_bass_kernel_spmd as _run

    nc = _bacc.Bacc("TRN2", target_bir_lowering=False, num_devices=1)
    arrays, args = {}, []
    for name in _INS:
        a = _np.ascontiguousarray(inputs[name])
        if name == "edge_weight1":
            a = a.reshape(-1)
        arrays[f"in_{name}"] = a
        args.append(nc.dram_tensor(f"in_{name}", a.shape, mybir.dt.from_np(a.dtype), kind="ExternalInput").ap())
    out = nc.dram_tensor("out_x", arrays["in_x"].shape, F32, kind="ExternalOutput").ap()
    build_program(nc, *args, out)
    return _run(nc, [arrays], core_ids=[0]).results[0]["out_x"]
```
